# Optimizing a Trainium2 kernel written in Bass

```python
import numpy as np
import jax
import jax.numpy as jnp

def _softmax(x, axis=-1):
    return jax.nn.softmax(x, axis=axis)

def _gelu(x):
    return jax.nn.gelu(x, approximate=True)

def _silu(x):
    return jax.nn.silu(x)

def _sigmoid(x):
    return jax.nn.sigmoid(x)

def _layernorm(x, axis=-1, eps=1e-05):
    m = jnp.mean(x, axis=axis, keepdims=True)
    v = jnp.var(x, axis=axis, keepdims=True)
    return (x - m) / jnp.sqrt(v + eps)

def _scatter_add(tgt, idx, src, axis=0):
    return tgt.at[idx].add(src)

def _segment_sum(src, seg, n):
    return jax.ops.segment_sum(src, seg, n)
kernel_name = 'mk_decoder_postln_d1_seqx_r8_867dbf'

def setup_inputs(seed: int=0):
    np.random.seed(seed)
    _w = jnp.asarray

    def _rec_inputs():
        import jax
        import jax.numpy as jnp
        _rk = jax.random.key(seed)
        x = 0.002226 + 0.9996 * jax.random.normal(jax.random.fold_in(_rk, 1), (64, 64, 128), jnp.float32)
        _lenS = 64 - jax.random.randint(jax.random.fold_in(_rk, 7), (64,), 0, max(1, 64 // 4) + 1, jnp.int32)
        _lenS2 = 64 - jax.random.randint(jax.random.fold_in(_rk, 8), (64,), 0, max(1, 64 // 4) + 1, jnp.int32)
        _ctx_1024P = jax.random.normal(jax.random.fold_in(_rk, 11), (64, 16, 128), jnp.float32)
        _ctx_1024c = jax.random.dirichlet(jax.random.fold_in(_rk, 511), 0.3 * jnp.ones((16,), jnp.float32), (64, 64))
        _ctx_1024t = jnp.einsum('bsk,bkd->bsd', _ctx_1024c, _ctx_1024P)
        _ctx_1024t = _ctx_1024t * jax.lax.rsqrt(jnp.mean(jnp.square(_ctx_1024t)) + 1e-12) * 0.953939
        ctx_1024 = -0.000125008 + 0.999885 * (_ctx_1024t + 0.3 * jax.random.normal(jax.random.fold_in(_rk, 611), (64, 64, 128), jnp.float32))
        return (x, ctx_1024)
    x, ctx_1024 = _rec_inputs()

    def _L0_attn_setup():
        import jax, jax.numpy as jnp
        import numpy as np
        DIM = 128
        D_INNER = 256
        D_STATE = 256
        DT_RANK = 256
        D_CONV = 3
        BATCH = 4
        SEQ = 256

        def _selective_scan(u, delta, A, Bp, Cp):
            delta_A = jnp.exp(jnp.einsum('blr,dr->bld', delta, A))
            delta_B_u = jnp.einsum('blr,dr->bld', delta, Bp) * u

            def step(carry, inp):
                xs, ds = carry
                dA_t, dBu_t, u_t = inp
                xs = dA_t * xs + dBu_t
                ds = ds + u_t * xs
                return ((xs, ds), (xs, ds))
            b = u.shape[0]
            init = (jnp.zeros((b, D_INNER), u.dtype), jnp.ones((b, D_INNER), u.dtype))
            seq = (jnp.moveaxis(delta_A, 1, 0), jnp.moveaxis(delta_B_u, 1, 0), jnp.moveaxis(u, 1, 0))
            _, (xs_seq, ds_seq) = jax.lax.scan(step, init, seq)
            xs_seq = jnp.moveaxis(xs_seq, 0, 1)
            ds_seq = jnp.moveaxis(ds_seq, 0, 1)
            x_c = jnp.einsum('bld,dr->blr', xs_seq, Cp)
            return (x_c, ds_seq)
        key = jax.random.key(seed)
        ks = jax.random.split(key, 9)
        f32 = jnp.float32
        x = jax.random.normal(ks[0], (BATCH, SEQ, DIM), f32)
        W_in = jax.random.normal(ks[1], (2 * D_INNER, DIM), f32) / np.sqrt(DIM)
        conv_w = jax.random.normal(ks[2], (D_INNER, 1, D_CONV), f32) / np.sqrt(D_CONV)
        conv_b = jax.random.normal(ks[3], (D_INNER,), f32) * 0.01
        W_dt = jax.random.normal(ks[4], (DT_RANK, D_INNER), f32) / np.sqrt(D_INNER)
        A_proj = jax.random.normal(ks[5], (D_INNER, D_STATE), f32) - 7.0
        B_proj = jax.random.normal(ks[6], (D_INNER, D_STATE), f32) * 0.05
        C_proj = jax.random.normal(ks[7], (D_INNER, D_STATE), f32) * 0.05
        W_out = jax.random.normal(ks[8], (DIM, D_INNER), f32) / np.sqrt(D_INNER)
        return {'x': x, 'W_in': W_in, 'conv_w': conv_w, 'conv_b': conv_b, 'W_dt': W_dt, 'A_proj': A_proj, 'B_proj': B_proj, 'C_proj': C_proj, 'W_out': W_out}
    _L0_attn_all = _L0_attn_setup()
    _L0_attn_in = {k: v for k, v in _L0_attn_all.items() if k in ('W_in', 'conv_w', 'conv_b', 'W_dt', 'A_proj', 'B_proj', 'C_proj', 'W_out')}
    del _L0_attn_all

    def _L0_xattn_setup():
        import jax, jax.numpy as jnp
        import numpy as np
        EPS = 1e-05

        def layer_norm(x, g, b):
            mu = jnp.mean(x, axis=-1, keepdims=True)
            var = jnp.var(x, axis=-1, keepdims=True)
            return (x - mu) * jax.lax.rsqrt(var + EPS) * g + b
        key = jax.random.key(seed)
        ks = jax.random.split(key, 8)
        dim, heads, dim_head = (128, 16, 64)
        inner = heads * dim_head
        b, n, m = (8, 512, 64)
        s = dim ** (-0.5)
        return {'x': jax.random.normal(ks[0], (b, n, dim), jnp.float32), 'latents': jax.random.normal(ks[1], (b, m, dim), jnp.float32), 'ln_m_g': jnp.ones((dim,), jnp.float32), 'ln_m_b': jnp.zeros((dim,), jnp.float32), 'ln_l_g': jnp.ones((dim,), jnp.float32), 'ln_l_b': jnp.zeros((dim,), jnp.float32), 'Wq': jax.random.normal(ks[2], (dim, inner), jnp.float32) * s, 'Wkv': jax.random.normal(ks[3], (dim, 2 * inner), jnp.float32) * s, 'Wout': jax.random.normal(ks[4], (inner, dim), jnp.float32) * s}
    _L0_xattn_all = _L0_xattn_setup()
    _L0_xattn_in = {k: v for k, v in _L0_xattn_all.items() if k in ('ln_m_g', 'ln_m_b', 'ln_l_g', 'ln_l_b', 'Wq', 'Wkv', 'Wout')}
    del _L0_xattn_all

    def _L0_ffn_setup():
        import jax, jax.numpy as jnp
        import numpy as np
        TOPK = 4
        key = jax.random.key(seed)
        ks = jax.random.split(key, 9)
        B, T, D = (4, 256, 128)
        E, H = (32, 128)
        HS = H * TOPK
        s = lambda k, shape, fan: jax.random.normal(k, shape, dtype=jnp.float32) / np.sqrt(fan)
        return {'x': jax.random.normal(ks[0], (B, T, D), dtype=jnp.float32), 'router_w': s(ks[1], (E, D), D), 'router_bias': jnp.zeros((E,), dtype=jnp.float32), 'gate_w': s(ks[2], (E, H, D), D), 'up_w': s(ks[3], (E, H, D), D), 'down_w': s(ks[4], (E, D, H), H), 'sgate_w': s(ks[5], (HS, D), D), 'sup_w': s(ks[6], (HS, D), D), 'sdown_w': s(ks[7], (D, HS), HS)}
    _L0_ffn_all = _L0_ffn_setup()
    _L0_ffn_in = {k: v for k, v in _L0_ffn_all.items() if k in ('router_w', 'router_bias', 'gate_w', 'up_w', 'down_w', 'sgate_w', 'sup_w', 'sdown_w')}
    del _L0_ffn_all
    return {'x': x, 'ctx_1024': ctx_1024, 'L0_attn_W_in': _L0_attn_in['W_in'], 'L0_attn_conv_w': _L0_attn_in['conv_w'], 'L0_attn_conv_b': _L0_attn_in['conv_b'], 'L0_attn_W_dt': _L0_attn_in['W_dt'], 'L0_attn_A_proj': _L0_attn_in['A_proj'], 'L0_attn_B_proj': _L0_attn_in['B_proj'], 'L0_attn_C_proj': _L0_attn_in['C_proj'], 'L0_attn_W_out': _L0_attn_in['W_out'], 'L0_xattn_ln_m_g': _L0_xattn_in['ln_m_g'], 'L0_xattn_ln_m_b': _L0_xattn_in['ln_m_b'], 'L0_xattn_ln_l_g': _L0_xattn_in['ln_l_g'], 'L0_xattn_ln_l_b': _L0_xattn_in['ln_l_b'], 'L0_xattn_Wq': _L0_xattn_in['Wq'], 'L0_xattn_Wkv': _L0_xattn_in['Wkv'], 'L0_xattn_Wout': _L0_xattn_in['Wout'], 'L0_ffn_router_w': _L0_ffn_in['router_w'], 'L0_ffn_router_bias': _L0_ffn_in['router_bias'], 'L0_ffn_gate_w': _L0_ffn_in['gate_w'], 'L0_ffn_up_w': _L0_ffn_in['up_w'], 'L0_ffn_down_w': _L0_ffn_in['down_w'], 'L0_ffn_sgate_w': _L0_ffn_in['sgate_w'], 'L0_ffn_sup_w': _L0_ffn_in['sup_w'], 'L0_ffn_sdown_w': _L0_ffn_in['sdown_w']}

def reference(x, ctx_1024, L0_attn_W_in, L0_attn_conv_w, L0_attn_conv_b, L0_attn_W_dt, L0_attn_A_proj, L0_attn_B_proj, L0_attn_C_proj, L0_attn_W_out, L0_xattn_ln_m_g, L0_xattn_ln_m_b, L0_xattn_ln_l_g, L0_xattn_ln_l_b, L0_xattn_Wq, L0_xattn_Wkv, L0_xattn_Wout, L0_ffn_router_w, L0_ffn_router_bias, L0_ffn_gate_w, L0_ffn_up_w, L0_ffn_down_w, L0_ffn_sgate_w, L0_ffn_sup_w, L0_ffn_sdown_w):
    import jax
    import jax.numpy as jnp

    def _L0_attn_ref(x, W_in, conv_w, conv_b, W_dt, A_proj, B_proj, C_proj, W_out):
        import jax, jax.numpy as jnp
        import numpy as np
        DIM = 128
        D_INNER = 256
        D_STATE = 256
        DT_RANK = 256
        D_CONV = 3
        BATCH = 4
        SEQ = 256

        def _selective_scan(u, delta, A, Bp, Cp):
            delta_A = jnp.exp(jnp.einsum('blr,dr->bld', delta, A))
            delta_B_u = jnp.einsum('blr,dr->bld', delta, Bp) * u

            def step(carry, inp):
                xs, ds = carry
                dA_t, dBu_t, u_t = inp
                xs = dA_t * xs + dBu_t
                ds = ds + u_t * xs
                return ((xs, ds), (xs, ds))
            b = u.shape[0]
            init = (jnp.zeros((b, D_INNER), u.dtype), jnp.ones((b, D_INNER), u.dtype))
            seq = (jnp.moveaxis(delta_A, 1, 0), jnp.moveaxis(delta_B_u, 1, 0), jnp.moveaxis(u, 1, 0))
            _, (xs_seq, ds_seq) = jax.lax.scan(step, init, seq)
            xs_seq = jnp.moveaxis(xs_seq, 0, 1)
            ds_seq = jnp.moveaxis(ds_seq, 0, 1)
            x_c = jnp.einsum('bld,dr->blr', xs_seq, Cp)
            return (x_c, ds_seq)
        xz = x @ W_in.T
        u, z = jnp.split(xz, 2, axis=-1)
        uc = jax.lax.conv_general_dilated(jnp.transpose(u, (0, 2, 1)), conv_w, window_strides=(1,), padding=[((D_CONV - 1) // 2,) * 2], dimension_numbers=('NCH', 'OIH', 'NCH'), feature_group_count=D_INNER)
        uc = uc + conv_b[None, :, None]
        u = jax.nn.silu(jnp.transpose(uc, (0, 2, 1)))
        A = -jnp.exp(A_proj)
        delta = jax.nn.softplus(u @ W_dt.T)
        x_c, d_acc = _selective_scan(u, delta, A, B_proj, C_proj)
        y = x_c * z * d_acc
        return y @ W_out.T

    def _L0_xattn_ref(x, latents, ln_m_g, ln_m_b, ln_l_g, ln_l_b, Wq, Wkv, Wout):
        import jax, jax.numpy as jnp
        import numpy as np
        EPS = 1e-05

        def layer_norm(x, g, b):
            mu = jnp.mean(x, axis=-1, keepdims=True)
            var = jnp.var(x, axis=-1, keepdims=True)
            return (x - mu) * jax.lax.rsqrt(var + EPS) * g + b
        heads, dim_head = (16, 64)
        scale = dim_head ** (-0.5)
        x = layer_norm(x, ln_m_g, ln_m_b)
        lat = layer_norm(latents, ln_l_g, ln_l_b)
        b, m, _ = lat.shape
        q = lat @ Wq
        kv_input = jnp.concatenate([x, lat], axis=1)
        kv = kv_input @ Wkv
        k, v = jnp.split(kv, 2, axis=-1)

        def split_heads(t):
            return t.reshape(t.shape[0], t.shape[1], heads, dim_head).transpose(0, 2, 1, 3)
        q, k, v = (split_heads(q), split_heads(k), split_heads(v))
        dots = jnp.einsum('bhid,bhjd->bhij', q, k) * scale
        attn = jax.nn.softmax(dots, axis=-1)
        out = jnp.einsum('bhij,bhjd->bhid', attn, v)
        out = out.transpose(0, 2, 1, 3).reshape(b, m, heads * dim_head)
        return out @ Wout

    def _L0_ffn_ref(x, router_w, router_bias, gate_w, up_w, down_w, sgate_w, sup_w, sdown_w):
        import jax, jax.numpy as jnp
        import numpy as np
        TOPK = 4
        B, T, D = x.shape
        flat = x.reshape(B * T, D)
        logits = flat.astype(jnp.float32) @ router_w.T + router_bias
        scores = jax.nn.softmax(logits, axis=-1)
        topk_scores, topk_idx = jax.lax.top_k(scores, TOPK)
        topk_scores = topk_scores / jnp.clip(topk_scores.sum(axis=-1, keepdims=True), 1e-12, None)
        h = jax.nn.silu(jnp.einsum('nd,ehd->neh', flat, gate_w)) * jnp.einsum('nd,ehd->neh', flat, up_w)
        expert_out = jnp.einsum('neh,edh->ned', h, down_w)
        sel = jnp.take_along_axis(expert_out, topk_idx[:, :, None], axis=1)
        out = (sel * topk_scores.astype(flat.dtype)[:, :, None]).sum(axis=1)
        out = out + jax.nn.silu(flat @ sgate_w.T) * (flat @ sup_w.T) @ sdown_w.T
        return out.reshape(B, T, D)
    x = _layernorm(x + _L0_attn_ref(x, L0_attn_W_in, L0_attn_conv_w, L0_attn_conv_b, L0_attn_W_dt, L0_attn_A_proj, L0_attn_B_proj, L0_attn_C_proj, L0_attn_W_out), axis=-1)
    x = _layernorm(x + _L0_xattn_ref(ctx_1024, x, L0_xattn_ln_m_g, L0_xattn_ln_m_b, L0_xattn_ln_l_g, L0_xattn_ln_l_b, L0_xattn_Wq, L0_xattn_Wkv, L0_xattn_Wout), axis=-1)
    x = _layernorm(x + _L0_ffn_ref(x, L0_ffn_router_w, L0_ffn_router_bias, L0_ffn_gate_w, L0_ffn_up_w, L0_ffn_down_w, L0_ffn_sgate_w, L0_ffn_sup_w, L0_ffn_sdown_w), axis=-1)
    return x

_drawn_inputs = setup_inputs


def setup_inputs(seed=0):
    import zlib

    import numpy as np

    out = dict(_drawn_inputs(seed))
    spreads = {'L0_xattn_ln_m_g': (1.0, 0.2),
     'L0_xattn_ln_m_b': (0.0, 0.1),
     'L0_xattn_ln_l_g': (1.0, 0.2),
     'L0_xattn_ln_l_b': (0.0, 0.1),
     'L0_ffn_router_bias': (0.0, 0.1)}
    factors = {}
    for name, (base, spread) in spreads.items():
        noise = np.random.default_rng([zlib.crc32(name.encode()), seed]).standard_normal(out[name].shape)
        drawn = base * np.exp(spread * noise) if base else spread * noise
        out[name] = jnp.asarray(drawn.astype(out[name].dtype))
    for name, factor in factors.items():
        out[name] = (out[name] * factor).astype(out[name].dtype)
    return out
```

```python
from contextlib import ExitStack

import concourse.bass as bass
from concourse import mybir
import numpy as np

F32 = mybir.dt.float32
F32R = mybir.dt.float32r
I32 = mybir.dt.int32
U32 = mybir.dt.uint32
BF16 = mybir.dt.bfloat16
ACT = mybir.ActivationFunctionType
ALU = mybir.AluOpType
AX = mybir.AxisListType

P = 128
D = 128
BATCH, SEQ = 64, 64
TOKENS = BATCH * SEQ
TILES = TOKENS // P
DI = 256
NC_ = DI // P
MT = 512
MS = TOKENS // MT
MTT = MT // P
HEADS, DH = 16, 64
AB = 4
AT = AB * SEQ
AS = BATCH // AB
UNITS = 8
E, TOPK = 32, 4
HS = 512
TS = 16
SPLIT = (20, 12)
FIRST = (0, SPLIT[0])
XTG = tuple(-(-(TOPK * n + E - 1) // TS) * TS for n in SPLIT)
XT = sum(XTG)
EPS = 1e-5


def at_least(eng, sem, n):
    if not (isinstance(n, int) and n <= 0):
        eng.wait_ge(sem, n)


def dyn(ap, k, n=1):
    return ap[:, bass.ds(k * n, n), :] if n > 1 else ap[:, bass.ds(k, 1), :].rearrange("p a c -> p (a c)")


class Alloc:

    def __init__(self, nc, ctx):
        self.nc, self.ctx = nc, ctx

    def sb(self, name, shape, dt=F32):
        return self.ctx.enter_context(self.nc.sbuf_tensor(name, shape, dt))

    def ps(self, name, cols=512):
        return self.ctx.enter_context(self.nc.psum_tensor(name, [P, cols], F32))

    def sem(self, name):
        return self.ctx.enter_context(self.nc.semaphore(name))


def setup_phase(nc, t, w):
    with ExitStack() as ctx:
        a = Alloc(nc, ctx)
        win = a.sb("win_raw", [P, 4, P])
        wdt = a.sb("wdt_raw", [P, 2, DI])
        apr = a.sb("a_raw", [P, 2, DI])
        bpr = a.sb("b_raw", [P, 2, DI])
        wou = a.sb("wout_raw", [P, DI])
        rou = a.sb("router_raw", [P, P])
        wq = a.sb("wq_raw", [P, HEADS * DH])
        wkv = a.sb("wkv_raw", [P, 2 * HEADS * DH])
        wo = a.sb("xwout_raw", [P, 8, P])
        sg = a.sb("sgate_raw", [P, 4, P])
        su = a.sb("sup_raw", [P, 4, P])
        sd = a.sb("sdown_raw", [P, HS])
        wqT = a.sb("wqT", [P, 8, P])
        wkT = a.sb("wkT", [P, 8, P])
        wvT = a.sb("wvT", [P, 8, P])
        bank = [a.ps(f"setup_bank{i}") for i in range(8)]
        s_load = a.sem("s_load")
        s_zero = a.sem("s_zero")
        s_const = a.sem("s_const")
        s_tr = a.sem("s_tr")
        s_act = a.sem("s_act")
        s_dve = a.sem("s_dve")
        s_prod = a.sem("s_prod")
        s_hi = a.sem("s_hi")
        s_lo = a.sem("s_lo")
        block = ctx.enter_context(nc.Block())

        kv = wkv[:, :].rearrange("p (s c m) -> p s c m", s=2, m=P)
        groups = [
            ([win[:, c, :] for c in range(4)], t["winT"][:, :]),
            ([wdt[:, c, k * P:k * P + P] for k in range(2) for c in range(2)], t["wdtT"][:, :, :].rearrange("p a b -> p (a b)")),
            ([apr[:, c, k * P:k * P + P] for k in range(2) for c in range(2)], t["aT"][:, :, :].rearrange("p a b -> p (a b)")),
            ([bpr[:, c, k * P:k * P + P] for k in range(2) for c in range(2)], t["bT"][:, :, :].rearrange("p a b -> p (a b)")),
            ([wou[:, 0:P], wou[:, P:2 * P], rou[:, :]], t["woT_rT"][:, :, :].rearrange("p a b -> p (a b)")),
        ]
        for src, dst in ((wq[:, :].rearrange("p (c m) -> p c m", m=P), wqT), (kv[:, 0], wkT), (kv[:, 1], wvT)):
            for half in range(2):
                groups.append(([src[:, 4 * half + i, :] for i in range(4)], dst[:, 4 * half:4 * half + 4, :].rearrange("p a b -> p (a b)")))
        groups.append(([sg[:, c, :] for c in range(4)], t["sgT"][:, :]))
        groups.append(([su[:, c, :] for c in range(4)], t["suT"][:, :]))
        groups.append(([sd[:, c * P:c * P + P] for c in range(4)], t["sdT"][:, :, :].rearrange("p a b -> p (a b)")))
        NG = len(groups)
        EXP_GROUP = 2
        loads = [
            (win[:, :, :], w["W_in"].rearrange("(c p) d -> p c d", p=P)),
            (wdt[:, :, :], w["W_dt"].rearrange("(c p) d -> p c d", p=P)),
            (apr[:, :, :], w["A_proj"].rearrange("(c p) d -> p c d", p=P)),
            (bpr[:, :, :], w["B_proj"].rearrange("(c p) d -> p c d", p=P)),
            (t["cW"][:, :, :], w["C_proj"].rearrange("(c p) d -> p c d", p=P)),
            (wou[:, :], w["W_out"]),
            (wq[:, :], w["Wq"]),
            (wkv[:, :], w["Wkv"]),
            (wo[:, :, :], w["Wout"].rearrange("(c p) d -> p c d", p=P)),
            (sg[:, :, :], w["sgate_w"].rearrange("(c p) d -> p c d", p=P)),
            (su[:, :, :], w["sup_w"].rearrange("(c p) d -> p c d", p=P)),
            (sd[:, :], w["sdown_w"]),
            (t["conv_w"][:, :, :], w["conv_w"].rearrange("(c p) a k -> p c (a k)", p=P)),
            (t["conv_b"][:, 0:1], w["conv_b"][0:P].rearrange("(p o) -> p o", o=1)),
            (t["conv_b"][:, 1:2], w["conv_b"][P:DI].rearrange("(p o) -> p o", o=1)),
            (t["rbias"][:, :], w["router_bias"].partition_broadcast(P)),
        ]
        for name, lat, mem in (("gain", "ln_l_g", "ln_m_g"), ("shift", "ln_l_b", "ln_m_b")):
            for j in range(2):
                for i in (j, j + 2):
                    loads.append((t[name][j * 64:j * 64 + 64, i, :], w[lat].partition_broadcast(64)))
                    loads.append((t[name][64 - j * 64:128 - j * 64, i, :], w[mem].partition_broadcast(64)))

        @block.sync
        def _(sp):
            for dst, src in loads:
                sp.dma_start(dst, src).then_inc(s_load, 16)
            sp.wait_ge(s_zero, 1)
            sp.dma_start(rou[0:E, :], w["router_w"]).then_inc(s_load, 16)
            sp.wait_ge(s_load, 16 * (len(loads) + 1))

        @block.gpsimd
        def _(pl):
            pl.memset(rou[:, :], 0.0).then_inc(s_zero, 1)
            pl.memset(t["ident"][:, :], 0.0).then_inc(s_zero, 1)
            pl.memset(t["sel"][:, :, :], 0.0).then_inc(s_zero, 1)
            pl.memset(t["mhalf"][:, :], -0.5).then_inc(s_const, 1)
            pl.memset(t["eps"][:, :], EPS).then_inc(s_const, 1)
            pl.memset(t["one"][:, :], 1.0).then_inc(s_const, 1)
            pl.wait_ge(s_zero, 3)
            pl.affine_select(out=t["ident"][:, :], in_=t["ident"][:, :], compare_op=ALU.not_equal, fill=1.0,
                             base=0, pattern=[[-1, P]], channel_multiplier=1).then_inc(s_const, 1)
            pl.affine_select(out=t["sel"][:, :, :], in_=t["sel"][:, :, :], compare_op=ALU.not_equal, fill=-1.0,
                             base=0, pattern=[[-1, 4], [0, P]], channel_multiplier=1).then_inc(s_const, 1)

        @block.tensor
        def _(pe):
            pe.wait_ge(s_const, 5)
            pe.wait_ge(s_load, 16 * (len(loads) + 1))
            for g, (srcs, _) in enumerate(groups):
                if g >= 8:
                    pe.wait_ge(s_act if g % 2 == 0 else s_dve, (g - 8) // 2 + 1)
                for i, src in enumerate(srcs):
                    last = pe.transpose(bank[g % 8][:, i * P:i * P + P], src, t["ident"][:, :])
                last.then_inc(s_tr, 1)
            pe.wait_ge(s_act, (NG + 1) // 2)
            pe.wait_ge(s_dve, NG // 2)
            for n in range(8):
                lhs, rhs = (wqT, wkT) if n < 4 else (wvT, wo)
                half, j = n % 4 // 2, n % 2
                for i in range(4):
                    c = 4 * half + i
                    last = pe.matmul(bank[n][:, i * P:i * P + P], lhs[64 * j:64 * j + 64, c, :], rhs[64 * j:64 * j + 64, c, :],
                                     start=True, stop=True)
                last.then_inc(s_prod, 1)

        def heads(ap, n):
            half, j = n % 4 // 2, n % 2
            return ap[:, 8 * half:8 * half + 8, :].rearrange("p (c j) m -> p c j m", j=2)[:, :, j, :]

        @block.scalar
        def _(act):
            for g in range(0, NG, 2):
                act.wait_ge(s_tr, g + 1)
                n = len(groups[g][0]) * P
                act.activation(groups[g][1], bank[g % 8][:, 0:n], ACT.Exp if g == EXP_GROUP else ACT.Copy).then_inc(s_act, 1)
            act.wait_ge(s_const, 5)
            act.activation(t["ones_r"][:, :], t["ident"][:, :], ACT.Identity, scale=0.0, bias=t["one"][:, 0:1]).then_inc(s_act, 1)
            for n in range(8):
                act.wait_ge(s_prod, n + 1)
                act.activation(heads(t["m_hi"] if n < 4 else t["n_hi"], n), bank[n][:, :].rearrange("p (c m) -> p c m", m=P), ACT.Copy,
                               scale=DH ** -0.5 if n < 4 else 1.0).then_inc(s_hi, 1)

        @block.vector
        def _(dve):
            for g in range(1, NG, 2):
                dve.wait_ge(s_tr, g + 1)
                n = len(groups[g][0]) * P
                dve.tensor_copy(groups[g][1], bank[g % 8][:, 0:n]).then_inc(s_dve, 1)
            for n in range(8):
                dve.wait_ge(s_prod, n + 1)
                src = bank[n][:, :].rearrange("p (c m) -> p c m", m=P)
                if n < 4:
                    dve.wait_ge(s_hi, n + 1)
                    dve.scalar_tensor_tensor(out=heads(t["m_lo"], n), in0=src, scalar=DH ** -0.5,
                                             in1=heads(t["m_hi"], n).bitcast(F32), op0=ALU.mult, op1=ALU.subtract).then_inc(s_lo, 1)
                else:
                    dve.wait_ge(s_hi, n + 1)
                    dve.tensor_tensor(heads(t["n_lo"], n), src, heads(t["n_hi"], n).bitcast(F32), ALU.subtract).then_inc(s_lo, 1)


def mixer_phase(nc, t, x, xall, xs_rows):
    x_steps = x.rearrange("(k t p) d -> k p t d", t=MTT, p=P)
    with ExitStack() as ctx:
        a = Alloc(nc, ctx)
        W2 = NC_ * MT
        xin = [a.sb(f"xin{j}", [P, MTT, D]) for j in range(2)]
        xT = a.sb("xT", [P, MT])
        conv = a.sb("conv", [P, W2])
        us = [a.sb(f"us{j}", [P, W2]) for j in range(2)]
        zs = [a.sb(f"zs{j}", [P, W2]) for j in range(2)]
        clamp = a.sb("clamp", [P, W2])
        expd = a.sb("expd", [P, W2])
        logd = a.sb("logd", [P, W2])
        delta = a.sb("delta", [P, W2])
        dA = a.sb("dA", [P, W2])
        dBu = a.sb("dBu", [P, W2])
        xs = a.sb("xs", [P, W2])
        gx = a.sb("gx", [P, W2])
        acc = a.sb("acc", [P, W2])
        keep = a.sb("keep", [P, W2])
        xcz = a.sb("xcz", [P, W2])
        y = a.sb("y", [P, W2])
        h = a.sb("h", [P, MTT, D])
        st = a.sb("st", [P, MTT, 6])
        mv = a.sb("mv", [P, MTT, 2])
        spare = a.sb("spare", [P, 2])
        zero = a.sb("zero_rows", [P, 8 * D])
        s_zero, s_zr = a.sem("m_zero"), a.sem("m_zr")
        zr_rows = [r.rearrange("(z p r) d -> z p (r d)", p=P, r=8) for r in xs_rows]
        ve = a.sb("ve", [P, MTT])
        rstd = a.sb("rstd", [P, MTT])
        PU, PZ, PA, PB = (a.ps(n, W2) for n in ("PU", "PZ", "PA", "PB"))
        s_x = [a.sem(f"s_x{j}") for j in range(2)]
        s_xall = a.sem("s_xall")
        (s_fill, s_xTp, s_xT, s_up, s_zp, s_tap, s_cl, s_cr, s_zs, s_us, s_dtp, s_min, s_exp, s_ln, s_delta, s_ap, s_bp,
         s_dA, s_dBu, s_xs, s_gx, s_acc, s_cp, s_xcz, s_y, s_op, s_h, s_st, s_mv, s_ve, s_rstd, s_x1) = (
            a.sem("m_" + n) for n in ("fill", "xTp", "xT", "up", "zp", "tap", "cl", "cr", "zs", "us", "dtp", "min", "exp", "ln", "delta",
                                     "ap", "bp", "dA", "dBu", "xs", "gx", "acc", "cp", "xcz", "y", "op", "h", "st", "mv", "ve",
                                     "rstd", "x1"))
        block = ctx.enter_context(nc.Block())

        def seqs(ap):
            return ap.rearrange("p (s q) -> p s q", q=SEQ)

        def steady(eng, step):
            step(-1, 1, back=False, out=False)
            step(0, 0, out=False)
            with eng.Fori(0, (MS - 4) // 2) as i:
                step(i * 2 + 1, 1)
                step(i * 2 + 2, 0)
            step(MS - 3, 1)
            step(MS - 2, 0, turn=False)
            step(MS - 1, 1, turn=False, front=False)
            step(MS, 0, turn=False, front=False, back=False)

        @block.sync
        def _(sp):
            sp.dma_start(xin[0][:, :, :], x_steps[0]).then_inc(s_x[0], 16)
            sp.dma_start(xin[1][:, :, :], x_steps[1]).then_inc(s_x[1], 16)
            sp.dma_start(xall[:, :, :], x.rearrange("(t p) d -> p t d", p=P)).then_inc(s_xall, 16)
            sp.wait_ge(s_zero, 1)
            for g in range(2):
                for z in range(XTG[g] // 8):
                    sp.dma_start(zr_rows[g][z], zero[:, :]).then_inc(s_zr, 16)
            with sp.Fori(1, MS // 2) as i:
                for j in range(2):
                    sp.wait_ge(s_xTp, i * 2 + (j - 1))
                    sp.dma_start(xin[j][:, :, :], x_steps[bass.ds(i * 2 + j, 1)].rearrange("a p t d -> p (a t) d")).then_inc(s_x[j], 16)
            sp.wait_ge(s_x[0], 16 * MS // 2)
            sp.wait_ge(s_x[1], 16 * MS // 2)
            sp.wait_ge(s_zr, 16 * XT // 8)

        @block.tensor
        def _(pe):
            def turned(q, par):
                pe.wait_ge(s_x[par], (q - par) * 8 + 16)
                at_least(pe, s_cr, NC_ * q)
                for i in range(MTT):
                    last = pe.transpose(PU[:, i * P:i * P + P], xin[par][:, i, :], t["ident"][:, :])
                last.then_inc(s_xTp, 1)
            turned(0, 0)

            def step(k, par, turn=True, front=True, back=True, out=True):
                if front:
                    pe.wait_ge(s_xT, k + 2)
                    for c in range(NC_):
                        last = pe.matmul(PU[:, c * MT:c * MT + MT], t["winT"][:, c * P:c * P + P], xT[:, :], start=True, stop=True)
                    last.then_inc(s_up, 1)
                    at_least(pe, s_xcz, k)
                    for c in range(NC_):
                        last = pe.matmul(PZ[:, c * MT:c * MT + MT], t["winT"][:, DI + c * P:DI + c * P + P], xT[:, :], start=True, stop=True)
                    last.then_inc(s_zp, 1)
                if out:
                    pe.wait_ge(s_y, k)
                    at_least(pe, s_dBu, k)
                    for i in range(MTT):
                        for c in range(NC_):
                            last = pe.matmul(PB[:, i * P:i * P + P], y[:, c * MT + i * P:c * MT + i * P + P],
                                             t["woT_rT"][:, c, :], start=(c == 0), stop=(c == NC_ - 1))
                    last.then_inc(s_op, 1)
                if back:
                    pe.wait_ge(s_delta, k + 1)
                    for c in range(NC_):
                        for kk in range(NC_):
                            last = pe.matmul(PA[:, c * MT:c * MT + MT], t["aT"][:, kk, c * P:c * P + P], delta[:, kk * MT:kk * MT + MT],
                                             start=(kk == 0), stop=(kk == NC_ - 1))
                    last.then_inc(s_ap, 1)
                    at_least(pe, s_h, k)
                    for c in range(NC_):
                        for kk in range(NC_):
                            last = pe.matmul(PB[:, c * MT:c * MT + MT], t["bT"][:, kk, c * P:c * P + P], delta[:, kk * MT:kk * MT + MT],
                                             start=(kk == 0), stop=(kk == NC_ - 1))
                    last.then_inc(s_bp, 1)
                if front:
                    pe.wait_ge(s_us, k + 2)
                    if back:
                        pe.wait_ge(s_dA, k + 1)
                    for c in range(NC_):
                        for kk in range(NC_):
                            last = pe.matmul(PA[:, c * MT:c * MT + MT], t["wdtT"][:, kk, c * P:c * P + P], us[1 - par][:, kk * MT:kk * MT + MT],
                                             start=(kk == 0), stop=(kk == NC_ - 1))
                    last.then_inc(s_dtp, 1)
                if turn:
                    turned(k + 2, par)
                if back:
                    if front:
                        pe.wait_ge(s_zs, k + 2)
                    else:
                        pe.wait_ge(s_zs, MS)
                    pe.wait_ge(s_xs, k + 1)
                    for c in range(NC_):
                        for kk in range(NC_):
                            last = pe.matmul(PZ[:, c * MT:c * MT + MT], t["cW"][:, kk, c * P:c * P + P], xs[:, kk * MT:kk * MT + MT],
                                             start=(kk == 0), stop=(kk == NC_ - 1))
                    last.then_inc(s_cp, 1)
            steady(pe, step)

        @block.scalar
        def _(act):
            def turned(q):
                act.wait_ge(s_xTp, q + 1)
                act.activation(xT[:, :], PU[:, 0:MT], ACT.Copy).then_inc(s_xT, 1)
            turned(0)

            def step(k, par, turn=True, front=True, back=True, out=True):
                if front:
                    act.wait_ge(s_up, k + 2)
                    at_least(act, s_us, k + 1)
                    for c in range(NC_):
                        act.activation(conv[:, c * MT:c * MT + MT], PU[:, c * MT:c * MT + MT], ACT.Identity,
                                       bias=t["conv_b"][:, c:c + 1], scale=t["conv_w"][:, c, 1:2]).then_inc(s_tap, 1)
                    act.wait_ge(s_zp, k + 2)
                    act.activation(zs[1 - par][:, :], PZ[:, :], ACT.Copy).then_inc(s_zs, 1)
                    act.wait_ge(s_cr, NC_ * (k + 2))
                    at_least(act, s_gx, k)
                    act.activation(us[1 - par][:, :], conv[:, :], ACT.Silu).then_inc(s_us, 1)
                if back:
                    act.wait_ge(s_ap, k + 1)
                    at_least(act, s_xs, k)
                    if isinstance(k, int) and k == 0:
                        act.wait_ge(s_fill, 2)
                    act.activation(seqs(dA[:, :])[:, :, 1:SEQ], seqs(PA[:, :])[:, :, 1:SEQ], ACT.Exp, scale=-1.0).then_inc(s_dA, 1)
                if turn:
                    turned(k + 2)
                if front:
                    act.wait_ge(s_min, k + 2)
                    at_least(act, s_ln, k + 1)
                    act.activation(expd[:, :], clamp[:, :], ACT.Exp).then_inc(s_exp, 1)
                    act.wait_ge(s_exp, k + 2)
                    act.activation(logd[:, :], expd[:, :], ACT.Ln, bias=1.0).then_inc(s_ln, 1)
            steady(act, step)

        @block.gpsimd
        def _(pl):
            pl.memset(zero[:, :], 0.0).then_inc(s_zero, 1)
            pl.memset(dA[:, :], 0.0).then_inc(s_fill, 1)
            pl.memset(keep[:, :], 1.0).then_inc(s_fill, 1)
            pl.wait_ge(s_fill, 2)
            pl.memset(seqs(keep[:, :])[:, :, 0:1], 0.0).then_inc(s_fill, 1)

            def step(k, par, turn=True, front=True, back=True, out=True):
                if out:
                    pl.wait_ge(s_mv, MTT * k)
                    pl.tensor_tensor(ve[:, :], mv[:, :, 1], t["eps"][:, 0:MTT], ALU.add).then_inc(s_ve, 1)
                    pl.wait_ge(s_ve, k + 1)
                    pl.tensor_tensor(rstd[:, :], ve[:, :], t["mhalf"][:, 0:MTT], ALU.pow).then_inc(s_rstd, 1)
                if back:
                    pl.wait_ge(s_xs, k + 1)
                    at_least(pl, s_acc, k)
                    pl.tensor_tensor(gx[:, :], us[par][:, :], xs[:, :], ALU.mult).then_inc(s_gx, 1)
            steady(pl, step)

        @block.vector
        def _(dve):
            dve.memset(spare[:, 0:1], 0.0).then_inc(s_x1, 1)
            dve.memset(spare[:, 1:2], 0.0).then_inc(s_ve, 1)

            def step(k, par, turn=True, front=True, back=True, out=True):
                if front:
                    dve.wait_ge(s_tap, NC_ * (k + 2))
                    for c in range(NC_):
                        s, d = seqs(PU[:, c * MT:c * MT + MT]), seqs(conv[:, c * MT:c * MT + MT])
                        dve.scalar_tensor_tensor(out=d[:, :, 1:SEQ], in0=s[:, :, 0:SEQ - 1], scalar=t["conv_w"][:, c, 0:1],
                                                 in1=d[:, :, 1:SEQ], op0=ALU.mult, op1=ALU.add).then_inc(s_cl, 1)
                    dve.wait_ge(s_cl, NC_ * (k + 2))
                    for c in range(NC_):
                        s, d = seqs(PU[:, c * MT:c * MT + MT]), seqs(conv[:, c * MT:c * MT + MT])
                        dve.scalar_tensor_tensor(out=d[:, :, 0:SEQ - 1], in0=s[:, :, 1:SEQ], scalar=t["conv_w"][:, c, 2:3],
                                                 in1=d[:, :, 0:SEQ - 1], op0=ALU.mult, op1=ALU.add).then_inc(s_cr, 1)
                if out:
                    dve.wait_ge(s_op, k)
                    if isinstance(k, int) and k == 1:
                        dve.wait_ge(s_xall, 16)
                    dve.wait_ge(s_x1, MTT * (k - 1) + 1)
                    if not isinstance(k, int):
                        dve.wait_ge(s_xall, 16)
                    dve.tensor_tensor(h[:, :, :], PB[:, 0:MT].rearrange("p (a b) -> p a b", b=D), dyn(xall, k - 1, MTT), ALU.add).then_inc(s_h, 1)
                    dve.wait_ge(s_h, k)
                    for i in range(MTT):
                        dve.bn_stats(st[:, i, :], h[:, i, :]).then_inc(s_st, 1)
                    dve.wait_ge(s_st, MTT * k)
                    dve.wait_ge(s_ve, k)
                if back:
                    dve.wait_ge(s_bp, k + 1)
                    dve.wait_ge(s_us, k + 1)
                    at_least(dve, s_xs, k)
                    dve.tensor_tensor(dBu[:, :], PB[:, :], us[par][:, :], ALU.mult).then_inc(s_dBu, 1)
                if out:
                    for i in range(MTT):
                        dve.bn_aggr(mv[:, i, :], st[:, i, :]).then_inc(s_mv, 1)
                if back:
                    dve.wait_ge(s_dA, k + 1)
                    dve.wait_ge(s_dBu, k + 1)
                    at_least(dve, s_cp, k)
                    at_least(dve, s_gx, k)
                    dve.tensor_tensor_scan(xs[:, :], dA[:, :], dBu[:, :], 0.0, ALU.mult, ALU.add).then_inc(s_xs, 1)
                if front:
                    dve.wait_ge(s_dtp, k + 2)
                    at_least(dve, s_exp, k + 1)
                    dve.tensor_scalar(clamp[:, :], PA[:, :], 20.0, None, ALU.min).then_inc(s_min, 1)
                if back:
                    dve.wait_ge(s_gx, k + 1)
                    if isinstance(k, int) and k == 0:
                        dve.wait_ge(s_fill, 3)
                    at_least(dve, s_y, k)
                    dve.tensor_tensor_scan(acc[:, :], keep[:, :], gx[:, :], 0.0, ALU.mult, ALU.add).then_inc(s_acc, 1)
                if back:
                    dve.wait_ge(s_cp, k + 1)
                    dve.wait_ge(s_zs, k + 1)
                    dve.tensor_tensor(xcz[:, :], PZ[:, :], zs[par][:, :], ALU.mult).then_inc(s_xcz, 1)
                if front:
                    dve.wait_ge(s_ln, k + 2)
                    if back:
                        dve.wait_ge(s_bp, k + 1)
                    dve.tensor_tensor(delta[:, :], logd[:, :], PA[:, :], ALU.max).then_inc(s_delta, 1)
                if back:
                    dve.wait_ge(s_acc, k + 1)
                    dve.wait_ge(s_xcz, k + 1)
                    at_least(dve, s_op, k)
                    dve.scalar_tensor_tensor(out=y[:, :], in0=acc[:, :], scalar=1.0, in1=xcz[:, :], op0=ALU.add, op1=ALU.mult).then_inc(s_y, 1)
                if out:
                    dve.wait_ge(s_rstd, k)
                    dve.wait_ge(s_mv, MTT * k)
                    for i in range(MTT):
                        dve.tensor_scalar(dyn(xall, (k - 1) * MTT + i), h[:, i, :], mv[:, i, 0:1], rstd[:, i:i + 1],
                                          ALU.subtract, ALU.mult).then_inc(s_x1, 1)
            steady(dve, step)


def attention_phase(nc, t, ctx_in, xall):
    ctx_rows = ctx_in.rearrange("(k i j) q d -> j k q i d", k=AS, j=2)
    with ExitStack() as ctx:
        a = Alloc(nc, ctx)
        cin = [a.sb(f"cin{j}", [P, 2, D]) for j in range(2)]
        st = a.sb("a_st", [P, 4, 6])
        mv = a.sb("a_mv", [P, 4, 2])
        ve = a.sb("a_ve", [P, 4])
        rstd = a.sb("a_rstd", [P, 4])
        kvn = a.sb("kvn", [P, AB, D])
        kvg = a.sb("kvg", [P, AB, D])
        kvs = a.sb("kvs", [P, AB, D])
        kvtok = [a.sb(f"kvtok{j}", [P, AB, D + 4]) for j in range(2)]
        kvh = [a.sb(f"kvT_hi{j}", [P, AB * P], F32R) for j in range(2)]
        kvl = [a.sb(f"kvT_lo{j}", [P, AB * P], F32R) for j in range(2)]
        qh = [a.sb(f"q_hi{j}", [P, AB, HEADS, SEQ], F32R) for j in range(2)]
        ql = [a.sb(f"q_lo{j}", [P, AB, HEADS, SEQ], F32R) for j in range(2)]
        mx = [a.sb(f"mx{j}", [P, P]) for j in range(2)]
        mT = [a.sb(f"mT{j}", [4, 4, P], F32R) for j in range(2)]
        pr = [a.sb(f"probs{j}", [P, 512]) for j in range(2)]
        rec = a.sb("rec", [P, 4])
        on = [a.sb(f"on{j}", [P, 4, P]) for j in range(2)]
        of = [a.sb(f"oT_full{j}", [P, 8, SEQ]) for j in range(2)]
        oh = a.sb("oT_hi", [P, HEADS, AB, SEQ], F32R)
        ol = a.sb("oT_lo", [P, HEADS, AB, SEQ], F32R)
        res = a.sb("resT", [P, AT])
        h = a.sb("a_h", [P, 2, D])
        fst = a.sb("f_st", [P, 2, 6])
        fmv = a.sb("f_mv", [P, 2, 2])
        spare = a.sb("a_spare", [P, 2])
        fve = a.sb("f_ve", [P, 2])
        frs = a.sb("f_rstd", [P, 2])
        psS, psM, psT, psOT, psQ, psN = (a.ps("a_" + n) for n in ("S", "M", "T", "OT", "Q", "N"))
        psO = a.ps("a_O", 1024)
        s_c = [a.sem(f"a_c{j}") for j in range(2)]
        (s_init, s_st, s_mv, s_ve, s_rs, s_kvn, s_kvg, s_kvs, s_kvtok, s_kvp, s_kvh, s_kvl, s_qp, s_qh, s_ql, s_S, s_mx, s_mp, s_mT,
         s_T, s_P, s_O, s_rc, s_On, s_OTp, s_OTf, s_OT, s_OTl, s_Np, s_res, s_fp, s_h, s_fst, s_fmv, s_fve, s_frs, s_x2) = (
            a.sem("a_" + n) for n in ("init", "st", "mv", "ve", "rs", "kvn", "kvg", "kvs", "kvtok", "kvp", "kvh", "kvl", "qp", "qh", "ql",
                                     "S", "mx", "mp", "mT", "T", "P", "O", "rc", "On", "OTp", "OTf", "OT", "OTl", "Np", "res", "fp", "h", "fst",
                                     "fmv", "fve", "frs", "x2"))
        block = ctx.enter_context(nc.Block())

        def steady(eng, step):
            for k in range(-2, 2):
                step(k, k % 2)
            with eng.Fori(0, (AS - 4) // 2) as i:
                step(i * 2 + 2, 0)
                step(i * 2 + 3, 1)
            for k in range(AS - 2, AS + 2):
                step(k, k % 2)

        def active(k):
            if not isinstance(k, int):
                return (True,) * 5
            return tuple(0 <= k + d < AS for d in (2, 1, 0, -1, -2))

        def unit(k, par, u):
            _, front, core, tail, _ = active(k)
            if u >= UNITS:
                return k * UNITS + u, 1 - par, u - UNITS, front
            if u < 0:
                return k * UNITS + u, 1 - par, u + UNITS, tail
            return k * UNITS + u, par, u, core

        def piece(k, par, s):
            _, front, core, _, _ = active(k)
            return (k * UNITS + s + 6, 1 - par, s - 2, front) if s >= 2 else (k * UNITS + s + 6, par, s + 6, core)

        @block.sync
        def _(sp):
            def load(q, par):
                for j in range(2):
                    lo = 64 - 64 * j
                    src = ctx_rows[j][bass.ds(q, 1)].rearrange("a q i d -> q (a i) d")
                    sp.dma_start(cin[par][lo:lo + 64, :, :], src).then_inc(s_c[par], 16)
            load(0, 0)
            load(1, 1)
            with sp.Fori(1, AS // 2) as i:
                for par in range(2):
                    sp.wait_ge(s_kvn, (i * 2 + (par - 1)) * 8)
                    load(i * 2 + par, par)
            for par in range(2):
                sp.wait_ge(s_c[par], 32 * AS // 2)

        @block.tensor
        def _(pe):
            def step(k, par):
                prep, front, core, tail, fin = active(k)
                for s in range(UNITS):
                    n, p2, u, there = unit(k, par, s + 2)
                    if there:
                        b, g = u % AB, u // AB
                        pe.wait_ge(s_qh, (n - u) + 4 * g + 4)
                        at_least(pe, s_mx, n)
                        for c in range(4):
                            last = pe.matmul(psS[:, c * P:c * P + P],
                                             qh[p2][:, b, 8 * g + 2 * c:8 * g + 2 * c + 2, :].rearrange("p h q -> p (h q)"),
                                             kvh[p2][:, b * P:b * P + P], start=True, stop=True)
                        last.then_inc(s_S, 1)
                    n, p2, u, there = unit(k, par, s + 1)
                    if there:
                        b, g = u % AB, u // AB
                        pe.wait_ge(s_ql, (n - u) + 4 * g + 4)
                        at_least(pe, s_P, n)
                        pe.wait_ge(s_mT, n + 1)
                        rh = qh[p2][:, b, 8 * g:8 * g + 8, :].rearrange("p h q -> p (h q)")
                        rl = ql[p2][:, b, 8 * g:8 * g + 8, :].rearrange("p h q -> p (h q)")
                        kh, kl = kvh[p2][:, b * P:b * P + P], kvl[p2][:, b * P:b * P + P]
                        for i, (l, r) in enumerate(((kh, rh), (kh, rl), (kl, rh))):
                            pe.matmul(psT[:, :], l, r, start=(i == 0), stop=False)
                        pe.matmul(psT[:, :], t["ones_r"][0:4, :], mT[u % 2][:, :, :].rearrange("p c m -> p (c m)"),
                                  start=False, stop=True).then_inc(s_T, 1)
                    if s == 1 and fin:
                        pe.wait_ge(s_res, k - 1)
                        pe.wait_ge(s_h, k - 1)
                        pe.wait_ge(s_OT, k * UNITS if core or tail else AS * UNITS)
                        for i in range(2):
                            last = pe.transpose(psOT[:, i * P:i * P + P], res[:, i * P:i * P + P], t["ident"][:, :])
                        last.then_inc(s_fp, 1)
                    n, p2, i, there = piece(k, par, s)
                    if there:
                        if i == 0:
                            pe.wait_ge(s_kvl, k + 2)
                        else:
                            pe.wait_ge(s_ql, n)
                        lat = [m[p2][:, :].rearrange("p (t r q) -> p t r q", t=2, r=4)[:, :, 0:4:3, :] for m in (kvh, kvl)]
                        for j in range(2):
                            mh, ml = t["m_hi"][:, 2 * i + j, :], t["m_lo"][:, 2 * i + j, :]
                            for m, (l, r) in enumerate(((mh, lat[0]), (mh, lat[1]), (ml, lat[0]))):
                                last = pe.matmul(psQ[:, j * AT:j * AT + AT], l, r, start=(m == 0), stop=(m == 2))
                        last.then_inc(s_qp, 1)
                    n, p2, u, there = unit(k, par, s + 2)
                    if there:
                        pe.wait_ge(s_mx, n + 1)
                        at_least(pe, s_mT, n)
                        pe.transpose(psM[:, 0:P], mx[u % 2][:, :], t["ident"][:, :]).then_inc(s_mp, 1)
                    n, p2, u, there = unit(k, par, s)
                    if there:
                        b = u % AB
                        pe.wait_ge(s_P, n + 1)
                        at_least(pe, s_On, n)
                        if s == 0:
                            pe.wait_ge(s_kvtok, k + 1)
                        for c in range(4):
                            o = 512 * (c // 2) + (D + 1) * (c % 2)
                            last = pe.matmul(psO[:, o:o + D + 1], pr[u % 2][:, c * P:c * P + P], kvtok[p2][:, b, 0:D + 1], start=True, stop=True)
                        last.then_inc(s_O, 1)
                    if s == 1 and front:
                        pe.wait_ge(s_kvs, 2 * (k + 2))
                        at_least(pe, s_ql, (k + 1) * UNITS)
                        for b in range(AB):
                            last = pe.transpose(psQ[:, b * P:b * P + P], kvs[:, b, :], t["ident"][:, :])
                        last.then_inc(s_kvp, 1)
                    n, p2, u, there = unit(k, par, s - 1)
                    if there:
                        pe.wait_ge(s_On, n + 1)
                        at_least(pe, s_OT, n)
                        if s == 1 and fin:
                            pe.wait_ge(s_h, k)
                        for c in range(4):
                            last = pe.transpose(psOT[:, c * P:c * P + P], on[u % 2][:, c, :], t["ident"][:, :])
                        last.then_inc(s_OTp, 1)
                    hd = (2 * s + 6) % HEADS
                    if core if s >= 5 else tail:
                        if s == 5:
                            pe.wait_ge(s_OTl, k * UNITS + 4)
                            at_least(pe, s_res, k)
                        if s == 1:
                            pe.wait_ge(s_OTl, k * UNITS)
                        for j in range(2):
                            nh, nl = t["n_hi"][:, hd + j, :], t["n_lo"][:, hd + j, :]
                            o_hi, o_lo = (o[:, hd + j, :, :].rearrange("p b q -> p (b q)") for o in (oh, ol))
                            for m, (l, r) in enumerate(((nh, o_hi), (nh, o_lo), (nl, o_hi))):
                                last = pe.matmul(psN[:, 0:AT], l, r, start=(hd + j == 0 and m == 0), stop=(hd + j == HEADS - 1 and m == 2))
                        last.then_inc(s_Np, 1)
            steady(pe, step)

        @block.scalar
        def _(act):
            def step(k, par):
                prep, front, core, tail, fin = active(k)
                for s in range(UNITS):
                    n, p2, u, there = unit(k, par, s + 1)
                    if there:
                        act.wait_ge(s_T, n + 1)
                        act.activation(pr[u % 2][:, :], psT[:, :], ACT.Exp).then_inc(s_P, 1)
                    n, p2, i, there = piece(k, par, s)
                    if there:
                        act.wait_ge(s_qp, n + 1)
                        act.activation(qh[p2][:, :, 2 * i:2 * i + 2, :].rearrange("p b j q -> p j b q"),
                                       psQ[:, :].rearrange("p (j b q) -> p j b q", j=2, b=AB), ACT.Copy).then_inc(s_qh, 1)
                    if s == 1 and front:
                        act.wait_ge(s_kvp, k + 2)
                        act.activation(kvh[1 - par][:, :], psQ[:, :], ACT.Copy).then_inc(s_kvh, 1)
                    n, p2, u, there = unit(k, par, s - 1)
                    if there:
                        b, g = u % AB, u // AB
                        src = psOT[:, :].rearrange("p (h q) -> p h q", q=SEQ)
                        act.wait_ge(s_OTp, n + 1)
                        at_least(act, s_OTl, n - 1)
                        act.activation(of[u % 2][:, :, :], src, ACT.Copy).then_inc(s_OTf, 1)
                        if b == 0:
                            at_least(act, s_Np, n - 4)
                        act.activation(oh[:, 8 * g:8 * g + 8, b, :], src, ACT.Copy).then_inc(s_OT, 1)
                    if s == 4 and tail:
                        act.wait_ge(s_Np, k * UNITS)
                        act.activation(res[:, :], psN[:, 0:AT], ACT.Copy).then_inc(s_res, 1)
            steady(act, step)

        @block.gpsimd
        def _(pl):
            for j in range(2):
                pl.memset(mx[j][:, :], 0.0).then_inc(s_init, 1)
                pl.memset(kvtok[j][:, :, D:D + 1], 1.0).then_inc(s_init, 1)
            pl.wait_ge(s_init, 4)

            def step(k, par):
                _, front, _, _, _ = active(k)
                if front:
                    scaled(k + 1, 1)
                for s in range(UNITS):
                    n, p2, u, there = unit(k, par, s - 1)
                    if there:
                        b, g = u % AB, u // AB
                        pl.wait_ge(s_OTf, n + 1)
                        pl.wait_ge(s_OT, n + 1)
                        pl.tensor_tensor(ol[:, 8 * g:8 * g + 8, b, :], of[u % 2][:, :, :],
                                         oh[:, 8 * g:8 * g + 8, b, :].bitcast(F32), ALU.subtract).then_inc(s_OTl, 1)
                    around(k, par, s)

            def around(k, par, s):
                prep, front, core, tail, fin = active(k)
                if s == 0 and front:
                    pl.wait_ge(s_kvs, 2 * (k + 2))
                    at_least(pl, s_O, k * UNITS)
                    pl.tensor_tensor(kvtok[1 - par][:, :, 0:D], kvg[:, :, :], t["shift"][:, :, :], ALU.add).then_inc(s_kvtok, 1)
                if s == 3 and fin:
                    pl.wait_ge(s_fmv, 2 * (k - 1))
                    pl.tensor_tensor(fve[:, :], fmv[:, :, 1], t["eps"][:, 0:2], ALU.add).then_inc(s_fve, 1)
                    pl.wait_ge(s_fve, k - 1)
                    pl.tensor_tensor(frs[:, :], fve[:, :], t["mhalf"][:, 0:2], ALU.pow).then_inc(s_frs, 1)
                if s == 4 and prep:
                    pl.wait_ge(s_mv, 4 * (k + 3))
                    pl.tensor_tensor(ve[:, :], mv[:, :, 1], t["eps"][:, 0:4], ALU.add).then_inc(s_ve, 1)
                    pl.wait_ge(s_ve, k + 3)
                    pl.tensor_tensor(rstd[:, :], ve[:, :], t["mhalf"][:, 0:4], ALU.pow).then_inc(s_rs, 1)
                if s == 7 and prep:
                    scaled(k + 2, 0)

            def scaled(q, half):
                two = slice(2 * half, 2 * half + 2)
                pl.wait_ge(s_kvn, 8 * q + 4 * half + 4)
                at_least(pl, s_kvtok, q)
                pl.tensor_tensor(kvg[:, two, :], kvn[:, two, :], t["gain"][:, two, :], ALU.mult).then_inc(s_kvg, 1)
                pl.wait_ge(s_kvg, 2 * q + half + 1)
                at_least(pl, s_kvp, q)
                pl.tensor_tensor(kvs[:, two, :], kvg[:, two, :], t["shift"][:, two, :], ALU.add).then_inc(s_kvs, 1)
            steady(pl, step)

        @block.vector
        def _(dve):
            dve.wait_ge(s_init, 4)
            dve.memset(spare[:, 0:1], 0.0).then_inc(s_h, 1)
            dve.memset(spare[:, 1:2], 0.0).then_inc(s_x2, 1)

            def step(k, par):
                prep, front, core, tail, fin = active(k)
                for s in range(UNITS):
                    if s == 3 and fin:
                        dve.wait_ge(s_fst, 2 * (k - 1))
                    if s == 4 and prep:
                        dve.wait_ge(s_st, 4 * (k + 3))
                    n, p2, u, there = unit(k, par, s + 2)
                    if there:
                        dve.wait_ge(s_S, n + 1)
                        dve.tensor_reduce(mx[u % 2][:, 0:4], psS[:, :].rearrange("p (c m) -> p c m", m=P), AX.X, ALU.max).then_inc(s_mx, 1)
                    if s == 3 and fin:
                        for i in range(2):
                            dve.bn_aggr(fmv[:, i, :], fst[:, i, :]).then_inc(s_fmv, 1)
                    if s == 4 and prep:
                        for i in range(4):
                            dve.bn_aggr(mv[:, i, :], st[:, i, :]).then_inc(s_mv, 1)
                    if s == 1 and fin:
                        dve.wait_ge(s_fp, k - 1)
                        dve.wait_ge(s_x2, 2 * (k - 2) + 1)
                        dve.tensor_tensor(h[:, :, :], psOT[:, 0:AT].rearrange("p (a b) -> p a b", b=D), dyn(xall, k - 2, 2), ALU.add).then_inc(s_h, 1)
                    n, p2, u, there = unit(k, par, s + 2)
                    if there:
                        dve.wait_ge(s_mp, n + 1)
                        dve.tensor_tensor(mT[u % 2][:, :, :], t["sel"][0:4, :, :],
                                          psM[0:4, 0:P].rearrange("p (o m) -> p o m", o=1).broadcast_to([4, 4, P]), ALU.mult).then_inc(s_mT, 1)
                    n, p2, i, there = piece(k, par, s)
                    if there:
                        dve.wait_ge(s_qh, n + 1)
                        v = lambda q: q[p2][:, :, 2 * i:2 * i + 2, :].rearrange("p b j q -> p j b q")
                        dve.tensor_tensor(v(ql), psQ[:, :].rearrange("p (j b q) -> p j b q", j=2, b=AB), v(qh).bitcast(F32),
                                          ALU.subtract).then_inc(s_ql, 1)
                    n, p2, u, there = unit(k, par, s)
                    if there:
                        dve.wait_ge(s_O, n + 1)
                        po = psO[:, :].rearrange("p (a r) -> p a r", a=2)[:, :, 0:2 * (D + 1)].rearrange("p a (j r) -> p a j r", j=2)
                        dve.reciprocal(rec[:, :].rearrange("p (a j) -> p a j", a=2), po[:, :, :, D]).then_inc(s_rc, 1)
                        dve.wait_ge(s_rc, n + 1)
                        dve.tensor_tensor(on[u % 2][:, :, :].rearrange("p (a j) d -> p a j d", a=2), po[:, :, :, 0:D],
                                          rec[:, :].rearrange("p (a j o) -> p a j o", a=2, o=1).broadcast_to([P, 2, 2, D]), ALU.mult).then_inc(s_On, 1)
                    if s == 1 and front:
                        dve.wait_ge(s_kvh, k + 2)
                        dve.tensor_tensor(kvl[1 - par][:, :], psQ[:, :], kvh[1 - par][:, :].bitcast(F32), ALU.subtract).then_inc(s_kvl, 1)
                    if s == 2 and fin:
                        dve.wait_ge(s_h, k)
                        for i in range(2):
                            dve.bn_stats(fst[:, i, :], h[:, i, :]).then_inc(s_fst, 1)
                    if s == 3 and prep:
                        dve.wait_ge(s_c[par], (k + 2 - par) * 16 + 32)
                        for i in range(2):
                            dve.bn_stats(st[:, i, :], dyn(xall, k * 2 + 4 + i)).then_inc(s_st, 1)
                        for i in range(2):
                            dve.bn_stats(st[:, 2 + i, :], cin[par][:, i, :]).then_inc(s_st, 1)
                    if s == 5 and fin:
                        dve.wait_ge(s_frs, k - 1)
                        for i in range(2):
                            dve.tensor_scalar(dyn(xall, k * 2 - 4 + i), h[:, i, :], fmv[:, i, 0:1], frs[:, i:i + 1],
                                              ALU.subtract, ALU.mult).then_inc(s_x2, 1)
                    if s >= 6 and prep:
                        i = s - 6
                        dve.wait_ge(s_rs, k + 3)
                        at_least(dve, s_kvg, 2 * (k + 2) - 1 + i)
                        for j in range(2):
                            r = slice(64 * j, 64 * j + 64)
                            dve.tensor_scalar(kvn[r, 2 * i + j, :], dyn(xall, k * 2 + 4 + i)[r], mv[r, i, 0:1], rstd[r, i:i + 1],
                                              ALU.subtract, ALU.mult).then_inc(s_kvn, 1)
                            dve.tensor_scalar(kvn[r, 2 * i + 1 - j, :], cin[par][r, i, :], mv[r, 2 + i, 0:1], rstd[r, 2 + i:3 + i],
                                              ALU.subtract, ALU.mult).then_inc(s_kvn, 1)
            steady(dve, step)


def router_phase(nc, t, w, xall, big, rows, xs_rows):
    G4 = 4
    NX = TILES // G4
    NW = 3 * E // G4
    with ExitStack() as ctx:
        a = Alloc(nc, ctx)
        x2T = a.sb("x2T", [P, TOKENS])
        raw = [a.sb(f"expert_raw{j}", [P, 3, G4, P]) for j in range(2)]
        logits = a.sb("logits", [P, TILES, E])
        top = a.sb("top", [P, TILES, 8])
        topi = a.sb("topi", [P, TILES, 8], U32)
        topf = a.sb("topf", [P, TILES, TOPK])
        dif = a.sb("dif", [P, TILES, TOPK])
        ex = a.sb("ex", [P, TILES, TOPK])
        sm = a.sb("sm", [P, TILES])
        rs = a.sb("rs", [P, TILES])
        iota_i = a.sb("iota_i", [P, E], I32)
        iota_e = a.sb("iota_e", [P, E])
        iota_ji = a.sb("iota_ji", [P, 2], I32)
        iota_j = a.sb("iota_j", [P, 2])
        oh = [a.sb(f"oh{k}", [P, TILES, E], BF16) for k in range(TOPK)]
        mask = [a.sb(f"mask{k}", [P, TILES, E], BF16) for k in range(TOPK - 1)]
        tri = a.sb("tri", [P, P], BF16)
        ones = a.sb("ones", [P, P], BF16)
        keep = [a.sb(f"keep_e{g}", [P, E, n]) for g, n in enumerate(SPLIT)]
        cnt = [a.sb(f"cnt{g}", [P, E, n]) for g, n in enumerate(SPLIT)]
        incl = [a.sb(f"incl{g}", [P, E, n]) for g, n in enumerate(SPLIT)]
        place = [a.sb(f"place{g}", [P, E, n]) for g, n in enumerate(SPLIT)]
        place2 = [a.sb(f"place2_{g}", [P, n, E]) for g, n in enumerate(SPLIT)]
        hit = [a.sb(f"hit{g}", [P, n, E]) for g, n in enumerate(SPLIT)]
        slotf = a.sb("slotf", [P, TOPK, TILES])
        tot1 = [a.sb(f"tot1{g}", [P, E], I32) for g in range(2)]
        tot2 = [a.sb(f"tot2{g}", [P, E], I32) for g in range(2)]
        nt = [a.sb(f"nt{g}", [P, E]) for g in range(2)]
        ends = [a.sb(f"ends{g}", [P, E]) for g in range(2)]
        onesE = a.sb("onesE", [P, E])
        base = [a.sb(f"base{g}", [P, E]) for g in range(2)]
        cmp_ = a.sb("cmp", [P, 2, E])
        eidp = a.sb("eidp", [P, 2])
        eidq = a.sb("eidq", [P, 2])
        sgs = [a.sb(f"sgs{j}", [P, MT]) for j in range(2)]
        hsT = [a.sb(f"hsT{j}", [P, 4, MT]) for j in range(2)]
        TB = [a.ps(f"r_TB{j}") for j in range(2)]
        LR = a.ps("r_LR", 1024)
        CC = a.ps("r_CC", 1024)
        EE = a.ps("r_EE")
        DD = a.ps("r_DD")
        s_raw = [a.sem(f"r_raw{j}") for j in range(2)]
        (s_fill, s_const, s_tp, s_ev, s_lg, s_L, s_top, s_ti, s_dif, s_ex, s_w, s_f, s_oh, s_mk, s_rk, s_cnt, s_incl,
         s_tiles, s_pl, s_hit, s_sl, s_slot, s_cmp, s_ei, s_ee, s_eid, s_sc, s_gp, s_sg, s_up, s_hs, s_dp, s_sh) = (
            a.sem("r_" + n) for n in ("fill", "const", "tp", "ev", "lg", "L", "top", "ti", "dif", "ex", "w", "f", "oh",
                                     "mk", "rk", "cnt", "incl", "tiles", "pl", "hit", "sl", "slot", "cmp", "ei",
                                     "ee", "eid", "sc", "gp", "sg", "up", "hs", "dp", "sh"))
        block = ctx.enter_context(nc.Block())
        raws = [w[n].rearrange("(g i) h d -> g h i d", i=G4) for n in ("gate_w", "up_w", "down_w")]

        def weight_dst(g):
            e4, kind = g // 3 * G4, g % 3
            return big["wd"][:, e4:e4 + G4, :] if kind == 2 else big["wgu"][:, e4:e4 + G4, kind * P:kind * P + P]

        @block.sync
        def _(sp):
            for g in range(E // G4):
                if g >= 2:
                    sp.wait_ge(s_tp, NX + 3 * (g - 1))
                for kind in range(3):
                    sp.dma_start(raw[g % 2][:, kind], raws[kind][g]).then_inc(s_raw[g % 2], 16)

        @block.gpsimd
        def _(pl):
            pl.memset(ones[:, :], 1.0).then_inc(s_fill, 1)
            pl.memset(tri[:, :], 1.0).then_inc(s_fill, 1)
            for g in range(2):
                pl.memset(keep[g][:, :, :], 1.0).then_inc(s_fill, 1)
            pl.memset(onesE[:, :], 1.0).then_inc(s_fill, 1)
            pl.memset(big["eid"][:, 0:1], 0).then_inc(s_const, 1)
            pl.iota(iota_i[:, :], pattern=[[1, E]], base=0, channel_multiplier=0).then_inc(s_fill, 1)
            pl.iota(iota_ji[:, :], pattern=[[0, 2]], base=0, channel_multiplier=1).then_inc(s_fill, 1)
            pl.wait_ge(s_fill, 7)
            pl.affine_select(out=tri[:, :], in_=tri[:, :], compare_op=ALU.is_gt, fill=0.0, base=0, pattern=[[1, P]],
                             channel_multiplier=-1).then_inc(s_const, 1)
            for g in range(2):
                pl.memset(keep[g][:, :, 0:1], 0.0).then_inc(s_const, 1)
            pl.tensor_copy(iota_e[:, :], iota_i[:, :]).then_inc(s_const, 1)
            pl.tensor_copy(iota_j[:, :], iota_ji[:, :]).then_inc(s_const, 1)
            pl.wait_ge(s_slot, 1)
            scatter(pl, 0, rows, xall, xs_rows[0], s_sc)
            pl.wait_ge(s_sc, 16 * SPLIT[0] * TOPK)

        @block.tensor
        def _(pe):
            def logit_group(g):
                pe.wait_ge(s_ev, g + 1)
                for i in range(G4 * g, G4 * g + G4):
                    last = pe.matmul(LR[:, i * E:i * E + E], x2T[:, i * P:i * P + P], t["woT_rT"][:, 2, 0:E], start=True, stop=True)
                last.then_inc(s_lg, 1)

            for g in range(NX):
                if g >= 2:
                    pe.wait_ge(s_ev, g - 1)
                for i in range(G4):
                    last = pe.transpose(TB[g % 2][:, i * P:i * P + P], xall[:, G4 * g + i, :], t["ident"][:, :])
                last.then_inc(s_tp, 1)
                if g >= 1:
                    logit_group(g - 1)
            logit_group(NX - 1)
            m = mask[2][:, :, :].rearrange("p t e -> p (t e)")
            for grp in range(2):
                for g in range(grp * NW // 2, (grp + 1) * NW // 2):
                    pe.wait_ge(s_raw[g // 3 % 2], 48 * (g // 3 // 2 + 1))
                    pe.wait_ge(s_ev, NX + g - 1)
                    for i in range(G4):
                        last = pe.transpose(TB[g % 2][:, i * P:i * P + P], raw[g // 3 % 2][:, g % 3, i, :], t["ident"][:, :])
                    last.then_inc(s_tp, 1)
                pe.wait_ge(s_const, 6)
                pe.wait_ge(s_mk, 3 * grp + 3)
                at_least(pe, s_pl, 3 * grp)
                lo, hi = FIRST[grp] * E, (FIRST[grp] + SPLIT[grp]) * E
                for o in (0, 512):
                    b, e = max(lo, o), min(hi, o + 512)
                    if b < e:
                        pe.matmul(LR[:, b:e], tri[:, :], m[:, b:e], start=True, stop=True)
                        last = pe.matmul(CC[:, b:e], ones[:, :], m[:, b:e], start=True, stop=True)
                last.then_inc(s_rk, 1)
            pe.wait_ge(s_ei, 2)
            for g in range(2):
                last = pe.matmul(EE[0:1, g * P:g * P + P], eidq[:, g:g + 1], t["ident"][:, :], start=True, stop=True)
            last.then_inc(s_ee, 1)
            pe.wait_ge(s_ev, NX + NW)
            pe.wait_ge(s_pl, 6)

            def step(k):
                xt = x2T[:, bass.ds(k * MT, MT)]
                for c in range(4):
                    at_least(pe, s_sg, k * 4 + c - 1)
                    pe.matmul(TB[c % 2][:, :], t["sgT"][:, c * P:c * P + P], xt, start=True, stop=True).then_inc(s_gp, 1)
                    at_least(pe, s_hs, k * 4 + c - 1)
                    pe.matmul(CC[:, c % 2 * 512:c % 2 * 512 + 512], t["suT"][:, c * P:c * P + P], xt, start=True, stop=True).then_inc(s_up, 1)

            def down(k, par):
                pe.wait_ge(s_hs, k * 4 + 4)
                at_least(pe, s_sh, k)
                for i in range(4):
                    for c in range(4):
                        last = pe.matmul(DD[:, i * P:i * P + P], hsT[par][:, c, i * P:i * P + P], t["sdT"][:, c, :], start=(c == 0), stop=(c == 3))
                last.then_inc(s_dp, 1)
            step(0)
            step(1)
            down(0, 0)
            with pe.Fori(1, NX // 2) as i:
                step(i * 2)
                down(i * 2 - 1, 1)
                step(i * 2 + 1)
                down(i * 2, 0)
            down(NX - 1, 1)

        @block.scalar
        def _(act):
            for g in range(NX):
                act.wait_ge(s_tp, g + 1)
                act.activation(x2T[:, g * MT:g * MT + MT], TB[g % 2][:, :], ACT.Copy).then_inc(s_ev, 1)
            for g in range(NW):
                act.wait_ge(s_tp, NX + g + 1)
                act.activation(weight_dst(g), TB[g % 2][:, :].rearrange("p (i m) -> p i m", m=P), ACT.Copy).then_inc(s_ev, 1)
            act.wait_ge(s_dif, 2)
            act.activation(ex[:, :, :], dif[:, :, :], ACT.Exp).then_inc(s_ex, 1)

            def step(k, par):
                for c in range(4):
                    act.wait_ge(s_gp, k * 4 + c + 1)
                    at_least(act, s_hs, k * 4 + c - 1)
                    act.activation(sgs[c % 2][:, :], TB[c % 2][:, :], ACT.Silu).then_inc(s_sg, 1)
            step(0, 0)
            step(1, 1)
            with act.Fori(1, NX // 2) as i:
                step(i * 2, 0)
                step(i * 2 + 1, 1)

        @block.vector
        def _(dve):
            bt = lambda ap, shape: ap.broadcast_to(shape)
            TE = [P, TILES, E]
            dve.wait_ge(s_lg, NX)
            dve.tensor_tensor(logits[:, :, :], LR[:, :].rearrange("p (t e) -> p t e", e=E),
                              bt(t["rbias"][:, :].rearrange("p (o e) -> p o e", o=1), TE), ALU.add).then_inc(s_L, 1)
            dve.wait_ge(s_L, 1)
            def route(g):
                T0, n = FIRST[g], SPLIT[g]
                tl = slice(T0, T0 + n)
                NE = [P, n, E]
                for i in range(T0, T0 + n):
                    dve.max(top[:, i, :], logits[:, i, :]).then_inc(s_top, 1)
                for i in range(T0, T0 + n):
                    dve.wait_ge(s_top, i + 1)
                    dve.max_index(topi[:, i, :], top[:, i, :], logits[:, i, :]).then_inc(s_ti, 1)
                dve.wait_ge(s_top, T0 + n)
                dve.tensor_tensor(dif[:, tl, :], top[:, tl, 0:TOPK], bt(top[:, tl, 0:1], [P, n, TOPK]), ALU.subtract).then_inc(s_dif, 1)
                dve.wait_ge(s_ti, T0 + n)
                dve.tensor_copy(topf[:, tl, :], topi[:, tl, 0:TOPK]).then_inc(s_f, 1)
                dve.wait_ge(s_const, 6)
                dve.wait_ge(s_f, g + 1)
                for k in range(TOPK):
                    dve.tensor_tensor(oh[k][:, tl, :], bt(iota_e[:, :].rearrange("p (o e) -> p o e", o=1), NE), bt(topf[:, tl, k:k + 1], NE),
                                      ALU.is_equal).then_inc(s_oh, 1)
                src = oh[0]
                for k in range(1, TOPK):
                    dve.wait_ge(s_oh, g * TOPK + k + 1)
                    if k > 1:
                        dve.wait_ge(s_mk, g * 3 + k - 1)
                    dve.tensor_tensor(mask[k - 1][:, tl, :], src[:, tl, :], oh[k][:, tl, :], ALU.add).then_inc(s_mk, 1)
                    src = mask[k - 1]
                dve.wait_ge(s_rk, g + 1)
                dve.tensor_copy(cnt[g][:, :, :], CC[:, T0 * E:(T0 + n) * E].rearrange("p (t e) -> p e t", e=E)).then_inc(s_cnt, 1)
                dve.wait_ge(s_cnt, g + 1)
                flat = lambda z: z[:, :, :].rearrange("p e t -> p (e t)")
                dve.tensor_tensor_scan(flat(incl[g]), flat(keep[g]), flat(cnt[g]), 0.0, ALU.mult, ALU.add).then_inc(s_incl, 1)
                dve.wait_ge(s_incl, g + 1)
                dve.tensor_scalar(tot1[g][:, :], incl[g][:, :, n - 1], float(P - 1), None, ALU.add).then_inc(s_tiles, 1)
                dve.wait_ge(s_tiles, 5 * g + 1)
                dve.tensor_scalar(tot2[g][:, :], tot1[g][:, :], 7, None, ALU.arith_shift_right).then_inc(s_tiles, 1)
                dve.wait_ge(s_tiles, 5 * g + 2)
                dve.tensor_copy(nt[g][:, :], tot2[g][:, :]).then_inc(s_tiles, 1)
                dve.wait_ge(s_tiles, 5 * g + 3)
                dve.tensor_tensor_scan(ends[g][:, :], onesE[:, :], nt[g][:, :], 0.0, ALU.mult, ALU.add).then_inc(s_tiles, 1)
                dve.wait_ge(s_tiles, 5 * g + 4)
                dve.tensor_tensor(base[g][:, :], ends[g][:, :], nt[g][:, :], ALU.subtract).then_inc(s_tiles, 1)
                dve.tensor_tensor(place[g][:, :, :], incl[g][:, :, :], cnt[g][:, :, :], ALU.subtract).then_inc(s_pl, 1)
                dve.wait_ge(s_tiles, 5 * g + 5)
                dve.wait_ge(s_pl, 3 * g + 1)
                dve.scalar_tensor_tensor(out=incl[g][:, :, :], in0=bt(base[g][:, :].rearrange("p (e o) -> p e o", o=1), [P, E, n]),
                                         scalar=float(P), in1=place[g][:, :, :], op0=ALU.mult, op1=ALU.add).then_inc(s_pl, 1)
                dve.wait_ge(s_pl, 3 * g + 2)
                dve.tensor_tensor(place2[g][:, :, :], LR[:, T0 * E:(T0 + n) * E].rearrange("p (t e) -> p t e", e=E),
                                  incl[g][:, :, :].rearrange("p e t -> p t e"), ALU.add).then_inc(s_pl, 1)
                dve.wait_ge(s_pl, 3 * g + 3)
                for k in range(TOPK):
                    at_least(dve, s_sl, g * TOPK + k)
                    dve.tensor_tensor(hit[g][:, :, :], oh[k][:, tl, :], place2[g][:, :, :], ALU.mult).then_inc(s_hit, 1)
                    dve.wait_ge(s_hit, g * TOPK + k + 1)
                    dve.tensor_reduce(slotf[:, k, tl], hit[g][:, :, :], AX.X, ALU.add).then_inc(s_sl, 1)
                dve.wait_ge(s_sl, (g + 1) * TOPK)
                dve.tensor_copy(rows[:, :, tl], slotf[:, :, tl]).then_inc(s_slot, 1)
            for g in range(2):
                route(g)
            for g in range(2):
                dve.tensor_scalar(cmp_[:, g, :], ends[g][:, :], iota_j[:, g:g + 1], None, ALU.is_le).then_inc(s_cmp, 1)
            dve.wait_ge(s_cmp, 2)
            dve.tensor_reduce(eidp[:, :], cmp_[:, :, :], AX.X, ALU.add).then_inc(s_ei, 1)
            dve.wait_ge(s_ei, 1)
            dve.tensor_scalar(eidq[:, :], eidp[:, :], float(E - 1), None, ALU.min).then_inc(s_ei, 1)
            dve.wait_ge(s_ex, 1)
            dve.tensor_reduce(sm[:, :], ex[:, :, :], AX.X, ALU.add).then_inc(s_w, 1)
            dve.wait_ge(s_w, 1)
            dve.reciprocal(rs[:, :], sm[:, :]).then_inc(s_w, 1)
            dve.wait_ge(s_w, 2)
            dve.tensor_tensor(big["wts"][:, :, :], ex[:, :, :], bt(rs[:, :].rearrange("p (t o) -> p t o", o=1), [P, TILES, TOPK]), ALU.mult).then_inc(s_w, 1)
            dve.wait_ge(s_ee, 1)
            for g in range(2):
                dve.tensor_copy(big["eid"][:, 1 + g * XTG[0]:1 + g * XTG[0] + XTG[g]], EE[0:1, g * P:g * P + XTG[g]]).then_inc(s_eid, 1)

            def step(k, par):
                for c in range(4):
                    dve.wait_ge(s_sg, k * 4 + c + 1)
                    dve.wait_ge(s_up, k * 4 + c + 1)
                    if c == 0:
                        at_least(dve, s_dp, k - 1)
                    dve.tensor_tensor(hsT[par][:, c, :], sgs[c % 2][:, :], CC[:, c % 2 * 512:c % 2 * 512 + 512], ALU.mult).then_inc(s_hs, 1)

            def down(k):
                dve.wait_ge(s_dp, k + 1)
                dve.tensor_tensor(dyn(big["sh"], k, 4), DD[:, :].rearrange("p (a b) -> p a b", b=D), dyn(xall, k, 4), ALU.add).then_inc(s_sh, 1)
            step(0, 0)
            step(1, 1)
            down(0)
            with dve.Fori(1, NX // 2) as i:
                step(i * 2, 0)
                down(i * 2 - 1)
                step(i * 2 + 1, 1)
                down(i * 2)
            down(NX - 1)


def scatter(pl, g, rows, xall, xs_rows, s_sc):
    for i in range(FIRST[g], FIRST[g] + SPLIT[g]):
        for k in range(TOPK):
            pl.indirect_dma_start(xs_rows[:, :], bass.IndirectOffsetOnAxis(ap=rows[:, k, i:i + 1], axis=0),
                                  xall[:, i, :], None).then_inc(s_sc, 16)


def gather(pl, i, rows, y_rows, dst, s_got):
    for k in range(TOPK):
        pl.indirect_dma_start(dst[:, k, :], None, y_rows[:, :],
                              bass.IndirectOffsetOnAxis(ap=rows[:, k, i:i + 1], axis=0)).then_inc(s_got, 16)


def experts_phase(nc, t, big, rows, xall, xs_rows, y_rows):
    G4 = 4
    NB = TS // G4
    NS = XT // TS
    NS0 = XTG[0] // TS
    xs_g = [r.rearrange("(g i p) d -> g p i d", i=G4, p=P) for r in xs_rows]
    y_g = [r.rearrange("(g i p) d -> g p i d", i=G4, p=P) for r in y_rows]
    with ExitStack() as ctx:
        a = Alloc(nc, ctx)
        xj = [a.sb(f"xj{j}", [P, G4, D]) for j in range(NB)]
        yj = [a.sb(f"yj{j}", [P, G4, D]) for j in range(NB)]
        xT = [a.sb(f"xjT{j}", [P, P]) for j in range(2)]
        sj = [a.sb(f"silu{j}", [P, P]) for j in range(2)]
        hj = [a.sb(f"hid{j}", [P, P]) for j in range(2)]
        hT = [a.sb(f"hidT{j}", [P, P]) for j in range(2)]
        psX, psG, psH, psY = ([a.ps(f"e_{n}{j}") for j in range(2)] for n in "XGHY")
        s_ld = [a.sem(f"e_ld{j}") for j in range(NB)]
        s_st = [a.sem(f"e_st{j}") for j in range(NB)]
        s_xp, s_x, s_g, s_si, s_h, s_hp, s_hT, s_yp, s_y, s_sc, s_got = (
            a.sem("e_" + n) for n in ("xp", "x", "g", "si", "h", "hp", "hT", "yp", "y", "sc", "got"))
        block = ctx.enter_context(nc.Block())

        def steady(eng, step):
            step(-1)
            step(0)
            with eng.Fori(1, NS - 1) as i:
                step(i)
            step(NS - 1)
            step(NS)

        def tile(k, s):
            n = k * TS + s
            first = k + s // TS
            return n, s % TS, not isinstance(k, int) or 0 <= first < NS

        @block.sync
        def _(sp):
            def step(k, load, store):
                for j in range(NB):
                    if load is not None:
                        at_least(sp, s_xp, k * TS + G4 * (j + 1))
                        src = xs_g[load][bass.ds((k + (1 - NS0 * load)) * NB + j, 1)]
                        sp.dma_start(xj[j][:, :, :], src.rearrange("a p i d -> p (a i) d")).then_inc(s_ld[j], 16)
                    if store is not None:
                        sp.wait_ge(s_y, k * TS + G4 * (j + 1))
                        dst = y_g[store][bass.ds((k - NS0 * store) * NB + j, 1)]
                        sp.dma_start(dst.rearrange("a p i d -> p (a i) d"), yj[j][:, :, :]).then_inc(s_st[j], 16)
            step(-1, 0, None)
            with sp.Fori(0, NS0 - 1) as i:
                step(i, 0, 0)
            sp.wait_ge(s_sc, 16 * TOPK * SPLIT[1])
            step(NS0 - 1, 1, 0)
            with sp.Fori(NS0, NS - 1) as i:
                step(i, 1, 1)
            step(NS - 1, None, 1)
            for j in range(NB):
                sp.wait_ge(s_st[j], 16 * NS)

        @block.gpsimd
        def _(pl):
            scatter(pl, 1, rows, xall, xs_rows[1], s_sc)
            for j in range(NB):
                pl.wait_ge(s_st[j], 16 * NS0)
            for i in range(SPLIT[0]):
                gather(pl, i, rows, y_rows[0], big["got"][:, i * TOPK:(i + 1) * TOPK, :], s_got)
            pl.wait_ge(s_got, 16 * TOPK * SPLIT[0])

        @block.tensor
        def _(pe):
            def step(k):
                before = isinstance(k, int) and k < 0
                first, count = (0, 2) if before else (k * TS - 1, TS + 3)
                if isinstance(k, int) and k >= NS - 1:
                    count = TS + 1 if k < NS else 1
                _, ids = nc.values_load_multi_w_load_instructions(
                    big["eid"][0:1, bass.ds(first + 1, count)], engines=[mybir.EngineType.PE], min_val=0, max_val=E - 1,
                    skip_runtime_bounds_check_because="the router keeps them in 0 .. E-1")

                def expert(n, s):
                    return ids[s - TS if before else s + 1]
                for s in range(TS):
                    n, u, there = tile(k, s + 3)
                    if there:
                        if u % G4 == 0:
                            pe.wait_ge(s_ld[u // G4], (n - u) * (16 // TS) + 16)
                        at_least(pe, s_x, n - 1)
                        pe.transpose(psX[u % 2][:, 0:P], xj[u // G4][:, u % G4, :], t["ident"][:, :]).then_inc(s_xp, 1)
                    n, u, there = tile(k, s + 2)
                    if there:
                        e = expert(n, s + 2)
                        pe.wait_ge(s_x, n + 1)
                        at_least(pe, s_h, n - 1)
                        pe.matmul(psG[u % 2][:, 0:2 * P], xT[u % 2][:, :], dyn(big["wgu"], e), start=True, stop=True).then_inc(s_g, 1)
                    n, u, there = tile(k, s)
                    if there:
                        pe.wait_ge(s_h, n + 1)
                        at_least(pe, s_hT, n - 1)
                        pe.transpose(psH[u % 2][:, 0:P], hj[u % 2][:, :], t["ident"][:, :]).then_inc(s_hp, 1)
                    n, u, there = tile(k, s - 1)
                    if there:
                        e = expert(n, s - 1)
                        pe.wait_ge(s_hT, n + 1)
                        at_least(pe, s_y, n - 1)
                        pe.matmul(psY[u % 2][:, 0:P], hT[u % 2][:, :], dyn(big["wd"], e), start=True, stop=True).then_inc(s_yp, 1)
            steady(pe, step)

        @block.scalar
        def _(act):
            def step(k):
                for s in range(TS):
                    n, u, there = tile(k, s + 3)
                    if there:
                        act.wait_ge(s_xp, n + 1)
                        at_least(act, s_g, n - 1)
                        act.activation(xT[u % 2][:, :], psX[u % 2][:, 0:P], ACT.Copy).then_inc(s_x, 1)
                    n, u, there = tile(k, s + 2)
                    if there:
                        act.wait_ge(s_g, n + 1)
                        at_least(act, s_h, n - 1)
                        act.activation(sj[u % 2][:, :], psG[u % 2][:, 0:P], ACT.Silu).then_inc(s_si, 1)
            steady(act, step)

        @block.vector
        def _(dve):
            def step(k):
                for s in range(TS):
                    n, u, there = tile(k, s + 2)
                    if there:
                        dve.wait_ge(s_si, n + 1)
                        at_least(dve, s_hp, n - 1)
                        dve.tensor_tensor(hj[u % 2][:, :], sj[u % 2][:, :], psG[u % 2][:, P:2 * P], ALU.mult).then_inc(s_h, 1)
                    n, u, there = tile(k, s)
                    if there:
                        dve.wait_ge(s_hp, n + 1)
                        at_least(dve, s_yp, n - 1)
                        dve.tensor_copy(hT[u % 2][:, :], psH[u % 2][:, 0:P]).then_inc(s_hT, 1)
                    n, u, there = tile(k, s - 1)
                    if there:
                        dve.wait_ge(s_yp, n + 1)
                        if u % G4 == 0:
                            at_least(dve, s_st[u // G4], (n - u) * (16 // TS))
                        dve.tensor_copy(yj[u // G4][:, u % G4, :], psY[u % 2][:, 0:P]).then_inc(s_y, 1)
            steady(dve, step)


def combine_phase(nc, t, big, rows, y_rows, out):
    G4 = 4
    NG = TILES // G4
    out_g = out.rearrange("(g i p) d -> g p i d", i=G4, p=P)
    with ExitStack() as ctx:
        a = Alloc(nc, ctx)
        got = [a.sb(f"got{j}", [P, TOPK, D]) for j in range(SPLIT[1])]
        acc = [a.sb(f"acc{j}", [P, G4, D]) for j in range(2)]
        st = [a.sb(f"c_st{j}", [P, G4, 6]) for j in range(2)]
        mv = [a.sb(f"c_mv{j}", [P, G4, 2]) for j in range(2)]
        ve = [a.sb(f"c_ve{j}", [P, G4]) for j in range(2)]
        rstd = [a.sb(f"c_rstd{j}", [P, G4]) for j in range(2)]
        ob = [a.sb(f"ob{j}", [P, G4, D]) for j in range(2)]
        s_got = [a.sem(f"c_got{j}") for j in range(SPLIT[1] // G4)]
        s_o = [a.sem(f"c_o{j}") for j in range(2)]
        s_acc, s_st, s_mv, s_ve, s_rs, s_ob = (a.sem("c_" + n) for n in ("acc", "st", "mv", "ve", "rs", "ob"))
        block = ctx.enter_context(nc.Block())

        @block.gpsimd
        def _(pl):
            def power(g):
                pl.wait_ge(s_mv, G4 * (g + 1))
                pl.tensor_tensor(ve[g % 2][:, :], mv[g % 2][:, :, 1], t["eps"][:, 0:G4], ALU.add).then_inc(s_ve, 1)
                pl.wait_ge(s_ve, g + 1)
                pl.tensor_tensor(rstd[g % 2][:, :], ve[g % 2][:, :], t["mhalf"][:, 0:G4], ALU.pow).then_inc(s_rs, 1)
            for j in range(SPLIT[1]):
                gather(pl, FIRST[1] + j, rows, y_rows[1], got[j], s_got[j // G4])
                if j % 2 == 1 and j // 2 < FIRST[1] // G4:
                    power(j // 2)
            for g in range(min(SPLIT[1] // 2, FIRST[1] // G4), NG):
                power(g)

        @block.vector
        def _(dve):
            def weigh(g, par):
                late = g * G4 >= FIRST[1]
                if late:
                    dve.wait_ge(s_got[g - FIRST[1] // G4], 16 * TOPK * G4)
                at_least(dve, s_ob, g * G4 - G4)
                for k in range(TOPK):
                    for j in range(G4):
                        i = g * G4 + j
                        rows_k = got[i - FIRST[1]][:, k, :] if late else big["got"][:, i * TOPK + k, :]
                        if k:
                            dve.wait_ge(s_acc, (g * TOPK + k - 1) * G4 + j + 1)
                        base = acc[par][:, j, :] if k else dyn(big["sh"], i)
                        w1 = big["wts"][:, bass.ds(i, 1), k:k + 1].rearrange("p a b -> p (a b)")
                        dve.scalar_tensor_tensor(out=acc[par][:, j, :], in0=rows_k, scalar=w1, in1=base,
                                                 op0=ALU.mult, op1=ALU.add).then_inc(s_acc, 1)
                dve.wait_ge(s_acc, g * G4 * TOPK + G4 * TOPK)
                for j in range(G4):
                    dve.bn_stats(st[par][:, j, :], acc[par][:, j, :]).then_inc(s_st, 1)

            def norm(g, par):
                dve.wait_ge(s_rs, g + 1)
                at_least(dve, s_o[par], (g - par) * 8)
                for j in range(G4):
                    dve.tensor_scalar(ob[par][:, j, :], acc[par][:, j, :], mv[par][:, j, 0:1], rstd[par][:, j:j + 1],
                                      ALU.subtract, ALU.mult).then_inc(s_ob, 1)

            def aggregate(g, par):
                for j in range(G4):
                    dve.bn_aggr(mv[par][:, j, :], st[par][:, j, :]).then_inc(s_mv, 1)
            for g in range(NG):
                weigh(g, g % 2)
                dve.wait_ge(s_st, G4 * (g + 1))
                aggregate(g, g % 2)
                if g >= 1:
                    norm(g - 1, (g - 1) % 2)
            norm(NG - 1, (NG - 1) % 2)

        @block.sync
        def _(sp):
            for g in range(NG):
                sp.wait_ge(s_ob, G4 * (g + 1))
                sp.dma_start(out_g[g], ob[g % 2][:, :, :]).then_inc(s_o[g % 2], 16)
            for j in range(2):
                sp.wait_ge(s_o[j], 16 * NG // 2)


def decoder(nc, x, ctx_in, w, out, stop_after=None):
    xf = x.rearrange("b s d -> (b s) d")
    outf = out.rearrange("b s d -> (b s) d")
    with ExitStack() as ctx:
        a = Alloc(nc, ctx)
        t = {
            "ident": a.sb("ident", [P, P]), "sel": a.sb("sel", [P, 4, P]), "ones_r": a.sb("ones_r", [P, P], F32R), "mhalf": a.sb("mhalf", [P, 8]),
            "one": a.sb("one", [P, 4]), "eps": a.sb("eps", [P, 8]),
            "woT_rT": a.sb("woT_rT", [P, 3, P]), "rbias": a.sb("rbias", [P, E]),
            "gain": a.sb("gain", [P, AB, P]), "shift": a.sb("shift", [P, AB, P]),
            "sgT": a.sb("sgT", [P, HS]), "suT": a.sb("suT", [P, HS]), "sdT": a.sb("sdT", [P, 4, P]),
        }
        xs_rows = [nc.dram_tensor(f"xs_rows{g}", [XTG[g] * P, D], F32, kind="Internal").ap() for g in range(2)]
        y_rows = [nc.dram_tensor(f"y_rows{g}", [XTG[g] * P, D], F32, kind="Internal").ap() for g in range(2)]
        xall = a.sb("xall", [P, TILES, D])
        with ExitStack() as heads:
            b = Alloc(nc, heads)
            for name, dt in (("m_hi", F32R), ("m_lo", F32R), ("n_hi", F32R), ("n_lo", F32R)):
                t[name] = b.sb(name, [P, HEADS, P], dt)
            with ExitStack() as mixer:
                m = Alloc(nc, mixer)
                for name, shape in (("winT", [P, 2 * DI]), ("wdtT", [P, 2, DI]), ("aT", [P, 2, DI]), ("bT", [P, 2, DI]),
                                    ("cW", [P, 2, DI]), ("conv_w", [P, 2, 3]), ("conv_b", [P, 2])):
                    t[name] = m.sb(name if "conv" not in name else name + "_sb", shape)
                setup_phase(nc, t, w)
                mixer_phase(nc, t, xf, xall, xs_rows)
            attention_phase(nc, t, ctx_in, xall)
        if stop_after:
            with ExitStack() as c2:
                s = Alloc(nc, c2).sem("s_dbg")
                block = c2.enter_context(nc.Block())

                @block.sync
                def _(sp):
                    sp.dma_start(outf.rearrange("(t p) d -> p t d", p=P), xall[:, :, :]).then_inc(s, 16)
                    sp.wait_ge(s, 16)
            return
        big = {
            "wgu": a.sb("wgu", [P, E, 2 * P]), "wd": a.sb("wd", [P, E, P]), "sh": a.sb("sh", [P, TILES, D]),
            "wts": a.sb("wts", [P, TILES, TOPK]), "eid": a.sb("eid", [1, 2 * P], I32),
        }
        rows = a.sb("rows", [P, TOPK, TILES], U32)
        router_phase(nc, t, w, xall, big, rows, xs_rows)
        big["got"] = a.sb("got", [P, TOPK * SPLIT[0], D])
        experts_phase(nc, t, big, rows, xall, xs_rows, y_rows)
        combine_phase(nc, t, big, rows, y_rows, outf)


_INS = ['x', 'ctx_1024', 'L0_attn_W_in', 'L0_attn_conv_w', 'L0_attn_conv_b', 'L0_attn_W_dt', 'L0_attn_A_proj', 'L0_attn_B_proj',
        'L0_attn_C_proj', 'L0_attn_W_out', 'L0_xattn_ln_m_g', 'L0_xattn_ln_m_b', 'L0_xattn_ln_l_g', 'L0_xattn_ln_l_b',
        'L0_xattn_Wq', 'L0_xattn_Wkv', 'L0_xattn_Wout', 'L0_ffn_router_w', 'L0_ffn_router_bias', 'L0_ffn_gate_w', 'L0_ffn_up_w',
        'L0_ffn_down_w', 'L0_ffn_sgate_w', 'L0_ffn_sup_w', 'L0_ffn_sdown_w']
STOP = None


def kernel(**inputs):
    import concourse.bacc as _bacc
    from concourse.bass_utils import run_bass_kernel_spmd as _run

    nc = _bacc.Bacc("TRN2", target_bir_lowering=False, num_devices=1)
    arrays, aps = {}, {}
    for name in _INS:
        arr = np.ascontiguousarray(inputs[name])
        arrays[f"in_{name}_dram"] = arr
        short = name.replace("L0_attn_", "").replace("L0_xattn_", "").replace("L0_ffn_", "")
        aps[short] = nc.dram_tensor(f"in_{name}_dram", arr.shape, mybir.dt.from_np(arr.dtype), kind="ExternalInput").ap()
    out = nc.dram_tensor("out_0_dram", (BATCH, SEQ, D), F32, kind="ExternalOutput").ap()
    decoder(nc, aps.pop("x"), aps.pop("ctx_1024"), aps, out, STOP)
    r = _run(nc, [arrays], core_ids=[0])
    return r.results[0]["out_0_dram"]
```

```python
from contextlib import ExitStack

import concourse.bass as bass
from concourse import mybir
import numpy as np

F32 = mybir.dt.float32
F32R = mybir.dt.float32r
I32 = mybir.dt.int32
U32 = mybir.dt.uint32
BF16 = mybir.dt.bfloat16
ACT = mybir.ActivationFunctionType
ALU = mybir.AluOpType
AX = mybir.AxisListType

P = 128
D = 128
BATCH, SEQ = 64, 64
TOKENS = BATCH * SEQ
TILES = TOKENS // P
DI = 256
NC_ = DI // P
MT = 512
MS = TOKENS // MT
MTT = MT // P
HEADS, DH = 16, 64
AB = 4
AT = AB * SEQ
AS = BATCH // AB
UNITS = 8
E, TOPK = 32, 4
HS = 512
TS = 16
SPLIT = (20, 12)
FIRST = (0, SPLIT[0])
XTG = tuple(-(-(TOPK * n + E - 1) // TS) * TS for n in SPLIT)
XT = sum(XTG)
EPS = 1e-5


def at_least(eng, sem, n):
    if not (isinstance(n, int) and n <= 0):
        eng.wait_ge(sem, n)


def dyn(ap, k, n=1):
    return ap[:, bass.ds(k * n, n), :] if n > 1 else ap[:, bass.ds(k, 1), :].rearrange("p a c -> p (a c)")


class Alloc:

    def __init__(self, nc, ctx):
        self.nc, self.ctx = nc, ctx

    def sb(self, name, shape, dt=F32):
        return self.ctx.enter_context(self.nc.sbuf_tensor(name, shape, dt))

    def ps(self, name, cols=512):
        return self.ctx.enter_context(self.nc.psum_tensor(name, [P, cols], F32))

    def sem(self, name):
        return self.ctx.enter_context(self.nc.semaphore(name))


def setup_phase(nc, t, w):
    with ExitStack() as ctx:
        a = Alloc(nc, ctx)
        win = a.sb("win_raw", [P, 4, P])
        wdt = a.sb("wdt_raw", [P, 2, DI])
        apr = a.sb("a_raw", [P, 2, DI])
        bpr = a.sb("b_raw", [P, 2, DI])
        wou = a.sb("wout_raw", [P, DI])
        rou = a.sb("router_raw", [P, P])
        wq = a.sb("wq_raw", [P, HEADS * DH])
        wkv = a.sb("wkv_raw", [P, 2 * HEADS * DH])
        wo = a.sb("xwout_raw", [P, 8, P])
        sg = a.sb("sgate_raw", [P, 4, P])
        su = a.sb("sup_raw", [P, 4, P])
        sd = a.sb("sdown_raw", [P, HS])
        wqT = a.sb("wqT", [P, 8, P])
        wkT = a.sb("wkT", [P, 8, P])
        wvT = a.sb("wvT", [P, 8, P])
        a_exp = a.sb("a_exp", [P, 2 * DI])
        bank = [a.ps(f"setup_bank{i}") for i in range(8)]
        s_load = [a.sem(f"s_load{j}") for j in range(2)]
        s_zero = a.sem("s_zero")
        s_const = a.sem("s_const")
        s_tr = a.sem("s_tr")
        s_act = a.sem("s_act")
        s_dve = a.sem("s_dve")
        s_prod = a.sem("s_prod")
        s_hi = a.sem("s_hi")
        block = ctx.enter_context(nc.Block())

        kv = wkv[:, :].rearrange("p (s c m) -> p s c m", s=2, m=P)
        groups = [
            ([win[:, c, :] for c in range(4)], t["winT"][0][:, :], t["winT"][1][:, :]),
            ([wdt[:, c, k * P:k * P + P] for k in range(2) for c in range(2)], t["wdtT"][:, :, :].rearrange("p a b -> p (a b)")),
            ([apr[:, c, k * P:k * P + P] for k in range(2) for c in range(2)], a_exp[:, :]),
            ([bpr[:, c, k * P:k * P + P] for k in range(2) for c in range(2)], *(b[:, :, :].rearrange("p a b -> p (a b)") for b in t["bT"])),
            ([wou[:, 0:P], wou[:, P:2 * P]], t["woT"][:, :, :].rearrange("p a b -> p (a b)")),
        ]
        FIRST_LOADED = len(groups)
        for src, dst in ((wq[:, :].rearrange("p (c m) -> p c m", m=P), wqT), (kv[:, 0], wkT), (kv[:, 1], wvT)):
            for half in range(2):
                groups.append(([src[:, 4 * half + i, :] for i in range(4)], dst[:, 4 * half:4 * half + 4, :].rearrange("p a b -> p (a b)")))
        groups.append(([sd[:, c * P:c * P + P] for c in range(4)], t["sdT"][:, :, :].rearrange("p a b -> p (a b)")))
        groups.append(([sg[:, c, :] for c in range(4)], t["sgT"][0][:, :], t["sgT"][1][:, :]))
        groups.append(([su[:, c, :] for c in range(4)], t["suT"][0][:, :], t["suT"][1][:, :]))
        groups.append(([rou[:, :]], t["rT"][:, 0, :], t["rT"][:, 1, :]))
        NG = len(groups)
        EXP_GROUP = 2
        on_act = [len(g) == 3 or i % 2 == 0 for i, g in enumerate(groups)]
        on_dve = [len(g) == 3 or i % 2 == 1 for i, g in enumerate(groups)]
        loads = [
            [(win[:, :, :], w["W_in"].rearrange("(c p) d -> p c d", p=P)),
             (wdt[:, :, :], w["W_dt"].rearrange("(c p) d -> p c d", p=P)),
             (apr[:, :, :], w["A_proj"].rearrange("(c p) d -> p c d", p=P)),
             (bpr[:, :, :], w["B_proj"].rearrange("(c p) d -> p c d", p=P)),
             (wou[:, :], w["W_out"])],
            [(wq[:, :], w["Wq"]),
             (wkv[:, :], w["Wkv"]),
             (wo[:, :, :], w["Wout"].rearrange("(c p) d -> p c d", p=P)),
             (sd[:, :], w["sdown_w"]),
             (sg[:, :, :], w["sgate_w"].rearrange("(c p) d -> p c d", p=P)),
             (su[:, :, :], w["sup_w"].rearrange("(c p) d -> p c d", p=P)),
             (t["cW"][:, :, :], w["C_proj"].rearrange("(c p) d -> p c d", p=P)),
             (t["conv_w"][:, :, :], w["conv_w"].rearrange("(c p) a k -> p c (a k)", p=P)),
             (t["conv_b"][:, 0:1], w["conv_b"][0:P].rearrange("(p o) -> p o", o=1)),
             (t["conv_b"][:, 1:2], w["conv_b"][P:DI].rearrange("(p o) -> p o", o=1))],
        ]
        loaded = (16 * len(loads[0]), 16 * (len(loads[1]) + 1))

        @block.sync
        def _(sp):
            for j in range(2):
                for dst, src in loads[j]:
                    sp.dma_start(dst, src).then_inc(s_load[j], 16)
            sp.wait_ge(s_zero, 1)
            sp.dma_start(rou[0:E, :], w["router_w"]).then_inc(s_load[1], 16)
            sp.wait_ge(s_load[1], loaded[1])

        @block.gpsimd
        def _(pl):
            pl.memset(rou[:, :], 0.0).then_inc(s_zero, 1)
            pl.memset(t["ident"][:, :], 0.0).then_inc(s_zero, 1)
            pl.memset(t["sel"][:, :, :], 0.0).then_inc(s_zero, 1)
            pl.memset(t["mhalf"][:, :], -0.5).then_inc(s_const, 1)
            pl.memset(t["eps"][:, :], EPS).then_inc(s_const, 1)
            pl.memset(t["one"][:, :], 1.0).then_inc(s_const, 1)
            pl.wait_ge(s_zero, 3)
            pl.affine_select(out=t["ident"][:, :], in_=t["ident"][:, :], compare_op=ALU.not_equal, fill=1.0,
                             base=0, pattern=[[-1, P]], channel_multiplier=1).then_inc(s_const, 1)
            pl.affine_select(out=t["sel"][:, :, :], in_=t["sel"][:, :, :], compare_op=ALU.not_equal, fill=-1.0,
                             base=0, pattern=[[-1, 4], [0, P]], channel_multiplier=1).then_inc(s_const, 1)

        @block.tensor
        def _(pe):
            pe.wait_ge(s_const, 5)
            pe.wait_ge(s_load[0], loaded[0])
            for g, group in enumerate(groups):
                if g == FIRST_LOADED:
                    pe.wait_ge(s_load[1], loaded[1])
                if g >= 8:
                    at_least(pe, s_act, sum(on_act[:g - 7]))
                    at_least(pe, s_dve, sum(on_dve[:g - 7]))
                for i, src in enumerate(group[0]):
                    last = pe.transpose(bank[g % 8][:, i * P:i * P + P], src, t["ident"][:, :])
                last.then_inc(s_tr, 1)
            pe.wait_ge(s_act, sum(on_act))
            pe.wait_ge(s_dve, sum(on_dve))
            for n in range(8):
                lhs, rhs = (wqT, wkT) if n < 4 else (wvT, wo)
                half, j = n % 4 // 2, n % 2
                for i in range(4):
                    c = 4 * half + i
                    last = pe.matmul(bank[n][:, i * P:i * P + P], lhs[64 * j:64 * j + 64, c, :], rhs[64 * j:64 * j + 64, c, :],
                                     start=True, stop=True)
                last.then_inc(s_prod, 1)

        def heads(ap, n):
            half, j = n % 4 // 2, n % 2
            return ap[:, 8 * half:8 * half + 8, :].rearrange("p (c j) m -> p c j m", j=2)[:, :, j, :]

        @block.scalar
        def _(act):
            for g in range(NG):
                if not on_act[g]:
                    continue
                act.wait_ge(s_tr, g + 1)
                n = len(groups[g][0]) * P
                act.activation(groups[g][1], bank[g % 8][:, 0:n], ACT.Exp if g == EXP_GROUP else ACT.Copy).then_inc(s_act, 1)
            act.wait_ge(s_const, 5)
            act.wait_ge(s_act, sum(on_act))
            act.activation(t["aT"][0][:, :, :].rearrange("p a b -> p (a b)"), a_exp[:, :], ACT.Copy).then_inc(s_act, 1)
            act.activation(t["ones_r"][:, :], t["ident"][:, :], ACT.Identity, scale=0.0, bias=t["one"][:, 0:1]).then_inc(s_act, 1)
            for n in range(8):
                act.wait_ge(s_prod, n + 1)
                act.activation(heads(t["m_hi"] if n < 4 else t["n_hi"], n), bank[n][:, :].rearrange("p (c m) -> p c m", m=P), ACT.Copy,
                               scale=DH ** -0.5 if n < 4 else 1.0).then_inc(s_hi, 1)

        @block.vector
        def _(dve):
            for g in range(NG):
                if not on_dve[g]:
                    continue
                dve.wait_ge(s_tr, g + 1)
                n = len(groups[g][0]) * P
                if len(groups[g]) == 3:
                    dve.wait_ge(s_act, sum(on_act[:g + 1]))
                    dve.tensor_tensor(groups[g][2], bank[g % 8][:, 0:n], groups[g][1].bitcast(F32), ALU.subtract).then_inc(s_dve, 1)
                else:
                    dve.tensor_copy(groups[g][1], bank[g % 8][:, 0:n]).then_inc(s_dve, 1)
            dve.wait_ge(s_act, sum(on_act) + 1)
            dve.tensor_tensor(t["aT"][1][:, :, :].rearrange("p a b -> p (a b)"), a_exp[:, :],
                              t["aT"][0][:, :, :].rearrange("p a b -> p (a b)").bitcast(F32), ALU.subtract).then_inc(s_dve, 1)
            for n in range(8):
                dve.wait_ge(s_prod, n + 1)
                src = bank[n][:, :].rearrange("p (c m) -> p c m", m=P)
                if n < 4:
                    dve.wait_ge(s_hi, n + 1)
                    dve.scalar_tensor_tensor(out=heads(t["m_lo"], n), in0=src, scalar=DH ** -0.5,
                                             in1=heads(t["m_hi"], n).bitcast(F32), op0=ALU.mult, op1=ALU.subtract).then_inc(s_dve, 1)
                else:
                    dve.wait_ge(s_hi, n + 1)
                    dve.tensor_tensor(heads(t["n_lo"], n), src, heads(t["n_hi"], n).bitcast(F32), ALU.subtract).then_inc(s_dve, 1)


def mixer_phase(nc, t, w, x, xall, xs_rows):
    x_steps = x.rearrange("(k t p) d -> k p t d", t=MTT, p=P)
    with ExitStack() as ctx:
        a = Alloc(nc, ctx)
        W2 = NC_ * MT
        xin = [a.sb(f"xin{j}", [P, MTT, D]) for j in range(2)]
        xTh, xTl = (a.sb(n, [P, MT], F32R) for n in ("xT_hi", "xT_lo"))
        dh, dl = (a.sb(n, [P, W2], F32R) for n in ("delta_hi", "delta_lo"))
        conv = a.sb("conv", [P, W2])
        us = [a.sb(f"us{j}", [P, W2]) for j in range(2)]
        zs = [a.sb(f"zs{j}", [P, W2]) for j in range(2)]
        clamp = a.sb("clamp", [P, W2])
        expd = a.sb("expd", [P, W2])
        logd = a.sb("logd", [P, W2])
        delta = a.sb("delta", [P, W2])
        dA = a.sb("dA", [P, W2])
        dBu = a.sb("dBu", [P, W2])
        xs = a.sb("xs", [P, W2])
        gx = a.sb("gx", [P, W2])
        acc = a.sb("acc", [P, W2])
        keep = a.sb("keep", [P, W2])
        xcz = a.sb("xcz", [P, W2])
        y = a.sb("y", [P, W2])
        h = a.sb("h", [P, MTT, D])
        st = a.sb("st", [P, MTT, 6])
        mv = a.sb("mv", [P, MTT, 2])
        spare = a.sb("spare", [P, 2])
        zero = a.sb("zero_rows", [P, 8 * D])
        s_zero, s_zr, s_gain = a.sem("m_zero"), a.sem("m_zr"), a.sem("m_gain")
        loads = [(t["rbias"][:, :], w["router_bias"].partition_broadcast(P))]
        for name, lat, mem in (("gain", "ln_l_g", "ln_m_g"), ("shift", "ln_l_b", "ln_m_b")):
            for j in range(2):
                for i in (j, j + 2):
                    loads.append((t[name][j * 64:j * 64 + 64, i, :], w[lat].partition_broadcast(64)))
                    loads.append((t[name][64 - j * 64:128 - j * 64, i, :], w[mem].partition_broadcast(64)))
        zr_rows = [r.rearrange("(z p r) d -> z p (r d)", p=P, r=8) for r in xs_rows]
        ve = a.sb("ve", [P, MTT])
        rstd = a.sb("rstd", [P, MTT])
        PU, PZ, PA, PB = (a.ps(n, W2) for n in ("PU", "PZ", "PA", "PB"))
        s_x = [a.sem(f"s_x{j}") for j in range(2)]
        s_xall = a.sem("s_xall")
        (s_fill, s_xTp, s_xT, s_xTl, s_dh, s_dl, s_up, s_zp, s_tap, s_cl, s_cr, s_zs, s_us, s_dtp, s_min, s_exp, s_ln, s_delta, s_ap, s_bp,
         s_dA, s_dBu, s_xs, s_gx, s_acc, s_cp, s_xcz, s_y, s_op, s_h, s_st, s_mv, s_ve, s_rstd, s_x1) = (
            a.sem("m_" + n) for n in ("fill", "xTp", "xT", "xTl", "dh", "dl", "up", "zp", "tap", "cl", "cr", "zs", "us", "dtp", "min", "exp", "ln", "delta",
                                     "ap", "bp", "dA", "dBu", "xs", "gx", "acc", "cp", "xcz", "y", "op", "h", "st", "mv", "ve",
                                     "rstd", "x1"))
        block = ctx.enter_context(nc.Block())

        def seqs(ap):
            return ap.rearrange("p (s q) -> p s q", q=SEQ)

        def steady(eng, step):
            step(-1, 1, back=False, out=False)
            step(0, 0, out=False)
            with eng.Fori(0, (MS - 4) // 2) as i:
                step(i * 2 + 1, 1)
                step(i * 2 + 2, 0)
            step(MS - 3, 1)
            step(MS - 2, 0, turn=False)
            step(MS - 1, 1, turn=False, front=False)
            step(MS, 0, turn=False, front=False, back=False)

        @block.sync
        def _(sp):
            sp.dma_start(xin[0][:, :, :], x_steps[0]).then_inc(s_x[0], 16)
            sp.dma_start(xin[1][:, :, :], x_steps[1]).then_inc(s_x[1], 16)
            sp.dma_start(xall[:, :, :], x.rearrange("(t p) d -> p t d", p=P)).then_inc(s_xall, 16)
            for dst, src in loads:
                sp.dma_start(dst, src).then_inc(s_gain, 16)
            sp.wait_ge(s_zero, 1)
            for g in range(2):
                for z in range(XTG[g] // 8):
                    sp.dma_start(zr_rows[g][z], zero[:, :]).then_inc(s_zr, 16)
            with sp.Fori(1, MS // 2) as i:
                for j in range(2):
                    sp.wait_ge(s_xTp, i * 2 + (j - 1))
                    sp.dma_start(xin[j][:, :, :], x_steps[bass.ds(i * 2 + j, 1)].rearrange("a p t d -> p (a t) d")).then_inc(s_x[j], 16)
            sp.wait_ge(s_x[0], 16 * MS // 2)
            sp.wait_ge(s_x[1], 16 * MS // 2)
            sp.wait_ge(s_zr, 16 * XT // 8)
            sp.wait_ge(s_gain, 16 * len(loads))

        @block.tensor
        def _(pe):
            def turned(q, par):
                pe.wait_ge(s_x[par], (q - par) * 8 + 16)
                at_least(pe, s_cr, NC_ * q)
                for i in range(MTT):
                    last = pe.transpose(PU[:, i * P:i * P + P], xin[par][:, i, :], t["ident"][:, :])
                last.then_inc(s_xTp, 1)
            turned(0, 0)
            wh, wl = t["winT"]

            def product(out, c, chunks):
                pairs = [pair for chunk in chunks for pair in chunk]
                for m, (l, r) in enumerate(pairs):
                    last = pe.matmul(out[:, c * MT:c * MT + MT], l, r, start=(m == 0), stop=(m == len(pairs) - 1))
                return last

            def step(k, par, turn=True, front=True, back=True, out=True):
                if front:
                    pe.wait_ge(s_xTl, k + 2)
                    for c in range(NC_):
                        last = product(PU, c, [[(w[:, c * P:c * P + P], x[:, :]) for w, x in ((wh, xTh), (wh, xTl), (wl, xTh))]])
                    last.then_inc(s_up, 1)
                    at_least(pe, s_xcz, k)
                    for c in range(NC_):
                        last = product(PZ, c, [[(w[:, DI + c * P:DI + c * P + P], x[:, :]) for w, x in ((wh, xTh), (wh, xTl), (wl, xTh))]])
                    last.then_inc(s_zp, 1)
                if out:
                    pe.wait_ge(s_y, k)
                    at_least(pe, s_dBu, k)
                    for i in range(MTT):
                        for c in range(NC_):
                            last = pe.matmul(PB[:, i * P:i * P + P], y[:, c * MT + i * P:c * MT + i * P + P],
                                             t["woT"][:, c, :], start=(c == 0), stop=(c == NC_ - 1))
                    last.then_inc(s_op, 1)
                if back:
                    pe.wait_ge(s_dl, NC_ * (k + 1))
                    for c in range(NC_):
                        last = product(PA, c, [[(w[:, kk, c * P:c * P + P], x[:, kk * MT:kk * MT + MT])
                                                  for w, x in ((t["aT"][0], dh), (t["aT"][0], dl), (t["aT"][1], dh))] for kk in range(NC_)])
                    last.then_inc(s_ap, 1)
                    at_least(pe, s_h, k)
                    for c in range(NC_):
                        last = product(PB, c, [[(w[:, kk, c * P:c * P + P], x[:, kk * MT:kk * MT + MT])
                                                  for w, x in ((t["bT"][0], dh), (t["bT"][0], dl), (t["bT"][1], dh))] for kk in range(NC_)])
                    last.then_inc(s_bp, 1)
                if front:
                    pe.wait_ge(s_us, k + 2)
                    if back:
                        pe.wait_ge(s_dA, k + 1)
                    for c in range(NC_):
                        for kk in range(NC_):
                            last = pe.matmul(PA[:, c * MT:c * MT + MT], t["wdtT"][:, kk, c * P:c * P + P], us[1 - par][:, kk * MT:kk * MT + MT],
                                             start=(kk == 0), stop=(kk == NC_ - 1))
                    last.then_inc(s_dtp, 1)
                if turn:
                    turned(k + 2, par)
                if back:
                    if front:
                        pe.wait_ge(s_zs, k + 2)
                    else:
                        pe.wait_ge(s_zs, MS)
                    pe.wait_ge(s_xs, k + 1)
                    for c in range(NC_):
                        for kk in range(NC_):
                            last = pe.matmul(PZ[:, c * MT:c * MT + MT], t["cW"][:, kk, c * P:c * P + P], xs[:, kk * MT:kk * MT + MT],
                                             start=(kk == 0), stop=(kk == NC_ - 1))
                    last.then_inc(s_cp, 1)
            steady(pe, step)

        @block.scalar
        def _(act):
            def turned(q):
                act.wait_ge(s_xTp, q + 1)
                act.activation(xTh[:, :], PU[:, 0:MT], ACT.Copy).then_inc(s_xT, 1)
            turned(0)

            def step(k, par, turn=True, front=True, back=True, out=True):
                if front:
                    act.wait_ge(s_up, k + 2)
                    at_least(act, s_us, k + 1)
                    for c in range(NC_):
                        act.activation(conv[:, c * MT:c * MT + MT], PU[:, c * MT:c * MT + MT], ACT.Identity,
                                       bias=t["conv_b"][:, c:c + 1], scale=t["conv_w"][:, c, 1:2]).then_inc(s_tap, 1)
                    act.wait_ge(s_zp, k + 2)
                    act.activation(zs[1 - par][:, :], PZ[:, :], ACT.Copy).then_inc(s_zs, 1)
                    act.preload_act_table(ACT.Silu)
                    act.wait_ge(s_cr, NC_ * (k + 2))
                    at_least(act, s_gx, k)
                    act.activation(us[1 - par][:, :], conv[:, :], ACT.Silu).then_inc(s_us, 1)
                act.preload_act_table(ACT.Exp)
                if back:
                    act.wait_ge(s_ap, k + 1)
                    at_least(act, s_xs, k)
                    if isinstance(k, int) and k == 0:
                        act.wait_ge(s_fill, 2)
                    act.activation(seqs(dA[:, :])[:, :, 1:SEQ], seqs(PA[:, :])[:, :, 1:SEQ], ACT.Exp, scale=-1.0).then_inc(s_dA, 1)
                if turn:
                    turned(k + 2)
                if front:
                    act.wait_ge(s_min, k + 2)
                    at_least(act, s_ln, k + 1)
                    act.activation(expd[:, :], clamp[:, :], ACT.Exp).then_inc(s_exp, 1)
                    act.wait_ge(s_exp, k + 2)
                    act.activation(logd[:, :], expd[:, :], ACT.Ln, bias=1.0).then_inc(s_ln, 1)
                    act.wait_ge(s_delta, k + 2)
                    act.activation(dh[:, :], delta[:, :], ACT.Copy).then_inc(s_dh, 1)
            steady(act, step)

        @block.gpsimd
        def _(pl):
            pl.memset(zero[:, :], 0.0).then_inc(s_zero, 1)
            pl.memset(dA[:, :], 0.0).then_inc(s_fill, 1)
            pl.memset(keep[:, :], 1.0).then_inc(s_fill, 1)
            pl.wait_ge(s_fill, 2)
            pl.memset(seqs(keep[:, :])[:, :, 0:1], 0.0).then_inc(s_fill, 1)

            def step(k, par, turn=True, front=True, back=True, out=True):
                if out:
                    pl.wait_ge(s_mv, MTT * k)
                    pl.tensor_tensor(ve[:, :], mv[:, :, 1], t["eps"][:, 0:MTT], ALU.add).then_inc(s_ve, 1)
                    pl.wait_ge(s_ve, k + 1)
                    pl.tensor_tensor(rstd[:, :], ve[:, :], t["mhalf"][:, 0:MTT], ALU.pow).then_inc(s_rstd, 1)
                if back:
                    pl.wait_ge(s_xs, k + 1)
                    at_least(pl, s_acc, k)
                    pl.tensor_tensor(gx[:, :], us[par][:, :], xs[:, :], ALU.mult).then_inc(s_gx, 1)
                if front:
                    pl.wait_ge(s_dh, k + 2)
                    pl.tensor_tensor(dl[:, MT:], delta[:, MT:], dh[:, MT:].bitcast(F32), ALU.subtract).then_inc(s_dl, 1)
            steady(pl, step)

        @block.vector
        def _(dve):
            dve.memset(spare[:, 0:1], 0.0).then_inc(s_x1, 1)
            dve.memset(spare[:, 1:2], 0.0).then_inc(s_ve, 1)

            def turned(q):
                dve.wait_ge(s_xT, q + 1)
                dve.tensor_tensor(xTl[:, :], PU[:, 0:MT], xTh[:, :].bitcast(F32), ALU.subtract).then_inc(s_xTl, 1)
            turned(0)

            def step(k, par, turn=True, front=True, back=True, out=True):
                if front:
                    dve.wait_ge(s_tap, NC_ * (k + 2))
                    for c in range(NC_):
                        s, d = seqs(PU[:, c * MT:c * MT + MT]), seqs(conv[:, c * MT:c * MT + MT])
                        dve.scalar_tensor_tensor(out=d[:, :, 1:SEQ], in0=s[:, :, 0:SEQ - 1], scalar=t["conv_w"][:, c, 0:1],
                                                 in1=d[:, :, 1:SEQ], op0=ALU.mult, op1=ALU.add).then_inc(s_cl, 1)
                    dve.wait_ge(s_cl, NC_ * (k + 2))
                    for c in range(NC_):
                        s, d = seqs(PU[:, c * MT:c * MT + MT]), seqs(conv[:, c * MT:c * MT + MT])
                        dve.scalar_tensor_tensor(out=d[:, :, 0:SEQ - 1], in0=s[:, :, 1:SEQ], scalar=t["conv_w"][:, c, 2:3],
                                                 in1=d[:, :, 0:SEQ - 1], op0=ALU.mult, op1=ALU.add).then_inc(s_cr, 1)
                if out:
                    dve.wait_ge(s_op, k)
                    if isinstance(k, int) and k == 1:
                        dve.wait_ge(s_xall, 16)
                    dve.wait_ge(s_x1, MTT * (k - 1) + 1)
                    if not isinstance(k, int):
                        dve.wait_ge(s_xall, 16)
                    dve.tensor_tensor(h[:, :, :], PB[:, 0:MT].rearrange("p (a b) -> p a b", b=D), dyn(xall, k - 1, MTT), ALU.add).then_inc(s_h, 1)
                    dve.wait_ge(s_h, k)
                    for i in range(MTT):
                        dve.bn_stats(st[:, i, :], h[:, i, :]).then_inc(s_st, 1)
                    dve.wait_ge(s_st, MTT * k)
                    dve.wait_ge(s_ve, k)
                if back:
                    dve.wait_ge(s_bp, k + 1)
                    dve.wait_ge(s_us, k + 1)
                    at_least(dve, s_xs, k)
                    dve.tensor_tensor(dBu[:, :], PB[:, :], us[par][:, :], ALU.mult).then_inc(s_dBu, 1)
                if out:
                    for i in range(MTT):
                        dve.bn_aggr(mv[:, i, :], st[:, i, :]).then_inc(s_mv, 1)
                if back:
                    dve.wait_ge(s_dA, k + 1)
                    dve.wait_ge(s_dBu, k + 1)
                    at_least(dve, s_cp, k)
                    at_least(dve, s_gx, k)
                    dve.tensor_tensor_scan(xs[:, :], dA[:, :], dBu[:, :], 0.0, ALU.mult, ALU.add).then_inc(s_xs, 1)
                if front:
                    dve.wait_ge(s_dtp, k + 2)
                    at_least(dve, s_exp, k + 1)
                    dve.tensor_scalar(clamp[:, :], PA[:, :], 20.0, None, ALU.min).then_inc(s_min, 1)
                if back:
                    dve.wait_ge(s_gx, k + 1)
                    if isinstance(k, int) and k == 0:
                        dve.wait_ge(s_fill, 3)
                    at_least(dve, s_y, k)
                    dve.tensor_tensor_scan(acc[:, :], keep[:, :], gx[:, :], 0.0, ALU.mult, ALU.add).then_inc(s_acc, 1)
                if turn:
                    turned(k + 2)
                if back:
                    dve.wait_ge(s_cp, k + 1)
                    dve.wait_ge(s_zs, k + 1)
                    dve.tensor_tensor(xcz[:, :], PZ[:, :], zs[par][:, :], ALU.mult).then_inc(s_xcz, 1)
                if front:
                    dve.wait_ge(s_ln, k + 2)
                    if back:
                        dve.wait_ge(s_bp, k + 1)
                    dve.tensor_tensor(delta[:, :], logd[:, :], PA[:, :], ALU.max).then_inc(s_delta, 1)
                if back:
                    dve.wait_ge(s_acc, k + 1)
                    dve.wait_ge(s_xcz, k + 1)
                    at_least(dve, s_op, k)
                    dve.scalar_tensor_tensor(out=y[:, :], in0=acc[:, :], scalar=1.0, in1=xcz[:, :], op0=ALU.add, op1=ALU.mult).then_inc(s_y, 1)
                if out:
                    dve.wait_ge(s_rstd, k)
                    dve.wait_ge(s_mv, MTT * k)
                    for i in range(MTT):
                        dve.tensor_scalar(dyn(xall, (k - 1) * MTT + i), h[:, i, :], mv[:, i, 0:1], rstd[:, i:i + 1],
                                          ALU.subtract, ALU.mult).then_inc(s_x1, 1)
                if front:
                    dve.wait_ge(s_dh, k + 2)
                    dve.tensor_tensor(dl[:, 0:MT], delta[:, 0:MT], dh[:, 0:MT].bitcast(F32), ALU.subtract).then_inc(s_dl, 1)
            steady(dve, step)


def attention_phase(nc, t, ctx_in, xall):
    ctx_rows = ctx_in.rearrange("(k i j) q d -> j k q i d", k=AS, j=2)
    with ExitStack() as ctx:
        a = Alloc(nc, ctx)
        cin = [a.sb(f"cin{j}", [P, 2, D]) for j in range(2)]
        st = a.sb("a_st", [P, 4, 6])
        mv = a.sb("a_mv", [P, 4, 2])
        ve = a.sb("a_ve", [P, 4])
        rstd = a.sb("a_rstd", [P, 4])
        kvn = a.sb("kvn", [P, AB, D])
        kvg = a.sb("kvg", [P, AB, D])
        kvs = a.sb("kvs", [P, AB, D])
        kvtok = [a.sb(f"kvtok{j}", [P, AB, D + 4]) for j in range(2)]
        kvh = [a.sb(f"kvT_hi{j}", [P, AB * P], F32R) for j in range(2)]
        kvl = [a.sb(f"kvT_lo{j}", [P, AB * P], F32R) for j in range(2)]
        qh = [a.sb(f"q_hi{j}", [P, AB, HEADS, SEQ], F32R) for j in range(2)]
        ql = [a.sb(f"q_lo{j}", [P, AB, HEADS, SEQ], F32R) for j in range(2)]
        mx = [a.sb(f"mx{j}", [P, P]) for j in range(2)]
        mT = [a.sb(f"mT{j}", [4, 4, P], F32R) for j in range(2)]
        pr = [a.sb(f"probs{j}", [P, 512]) for j in range(2)]
        rec = a.sb("rec", [P, 4])
        on = [a.sb(f"on{j}", [P, 4, P]) for j in range(2)]
        of = [a.sb(f"oT_full{j}", [P, 8, SEQ]) for j in range(2)]
        oh = a.sb("oT_hi", [P, HEADS, AB, SEQ], F32R)
        ol = a.sb("oT_lo", [P, HEADS, AB, SEQ], F32R)
        res = a.sb("resT", [P, AT])
        h = a.sb("a_h", [P, 2, D])
        fst = a.sb("f_st", [P, 2, 6])
        fmv = a.sb("f_mv", [P, 2, 2])
        spare = a.sb("a_spare", [P, 2])
        fve = a.sb("f_ve", [P, 2])
        frs = a.sb("f_rstd", [P, 2])
        psS, psM, psT, psOT, psQ, psN = (a.ps("a_" + n) for n in ("S", "M", "T", "OT", "Q", "N"))
        psO = a.ps("a_O", 1024)
        s_c = [a.sem(f"a_c{j}") for j in range(2)]
        (s_init, s_st, s_mv, s_ve, s_rs, s_kvn, s_kvg, s_kvs, s_kvtok, s_kvp, s_kvh, s_kvl, s_qp, s_qh, s_ql, s_S, s_mx, s_mp, s_mT,
         s_T, s_P, s_O, s_rc, s_On, s_OTp, s_OTf, s_OT, s_OTl, s_Np, s_res, s_fp, s_h, s_fst, s_fmv, s_fve, s_frs, s_x2) = (
            a.sem("a_" + n) for n in ("init", "st", "mv", "ve", "rs", "kvn", "kvg", "kvs", "kvtok", "kvp", "kvh", "kvl", "qp", "qh", "ql",
                                     "S", "mx", "mp", "mT", "T", "P", "O", "rc", "On", "OTp", "OTf", "OT", "OTl", "Np", "res", "fp", "h", "fst",
                                     "fmv", "fve", "frs", "x2"))
        block = ctx.enter_context(nc.Block())

        def steady(eng, step):
            for k in range(-2, 2):
                step(k, k % 2)
            with eng.Fori(0, (AS - 4) // 2) as i:
                step(i * 2 + 2, 0)
                step(i * 2 + 3, 1)
            for k in range(AS - 2, AS + 2):
                step(k, k % 2)

        def active(k):
            if not isinstance(k, int):
                return (True,) * 5
            return tuple(0 <= k + d < AS for d in (2, 1, 0, -1, -2))

        def unit(k, par, u):
            _, front, core, tail, _ = active(k)
            if u >= UNITS:
                return k * UNITS + u, 1 - par, u - UNITS, front
            if u < 0:
                return k * UNITS + u, 1 - par, u + UNITS, tail
            return k * UNITS + u, par, u, core

        def piece(k, par, s):
            _, front, core, _, _ = active(k)
            return (k * UNITS + s + 6, 1 - par, s - 2, front) if s >= 2 else (k * UNITS + s + 6, par, s + 6, core)

        @block.sync
        def _(sp):
            def load(q, par):
                for j in range(2):
                    lo = 64 - 64 * j
                    src = ctx_rows[j][bass.ds(q, 1)].rearrange("a q i d -> q (a i) d")
                    sp.dma_start(cin[par][lo:lo + 64, :, :], src).then_inc(s_c[par], 16)
            load(0, 0)
            load(1, 1)
            with sp.Fori(1, AS // 2) as i:
                for par in range(2):
                    sp.wait_ge(s_kvn, (i * 2 + (par - 1)) * 8)
                    load(i * 2 + par, par)
            for par in range(2):
                sp.wait_ge(s_c[par], 32 * AS // 2)

        @block.tensor
        def _(pe):
            def step(k, par):
                prep, front, core, tail, fin = active(k)
                for s in range(UNITS):
                    n, p2, u, there = unit(k, par, s + 2)
                    if there:
                        b, g = u % AB, u // AB
                        pe.wait_ge(s_qh, (n - u) + 4 * g + 4)
                        at_least(pe, s_mx, n)
                        for c in range(4):
                            last = pe.matmul(psS[:, c * P:c * P + P],
                                             qh[p2][:, b, 8 * g + 2 * c:8 * g + 2 * c + 2, :].rearrange("p h q -> p (h q)"),
                                             kvh[p2][:, b * P:b * P + P], start=True, stop=True)
                        last.then_inc(s_S, 1)
                    n, p2, u, there = unit(k, par, s + 1)
                    if there:
                        b, g = u % AB, u // AB
                        pe.wait_ge(s_ql, (n - u) + 4 * g + 4)
                        at_least(pe, s_P, n)
                        pe.wait_ge(s_mT, n + 1)
                        rh = qh[p2][:, b, 8 * g:8 * g + 8, :].rearrange("p h q -> p (h q)")
                        rl = ql[p2][:, b, 8 * g:8 * g + 8, :].rearrange("p h q -> p (h q)")
                        kh, kl = kvh[p2][:, b * P:b * P + P], kvl[p2][:, b * P:b * P + P]
                        for i, (l, r) in enumerate(((kh, rh), (kh, rl), (kl, rh))):
                            pe.matmul(psT[:, :], l, r, start=(i == 0), stop=False)
                        pe.matmul(psT[:, :], t["ones_r"][0:4, :], mT[u % 2][:, :, :].rearrange("p c m -> p (c m)"),
                                  start=False, stop=True).then_inc(s_T, 1)
                    if s == 1 and fin:
                        pe.wait_ge(s_res, k - 1)
                        pe.wait_ge(s_h, k - 1)
                        pe.wait_ge(s_OT, k * UNITS if core or tail else AS * UNITS)
                        for i in range(2):
                            last = pe.transpose(psOT[:, i * P:i * P + P], res[:, i * P:i * P + P], t["ident"][:, :])
                        last.then_inc(s_fp, 1)
                    n, p2, i, there = piece(k, par, s)
                    if there:
                        if i == 0:
                            pe.wait_ge(s_kvl, k + 2)
                        else:
                            pe.wait_ge(s_ql, n)
                        lat = [m[p2][:, :].rearrange("p (t r q) -> p t r q", t=2, r=4)[:, :, 0:4:3, :] for m in (kvh, kvl)]
                        for j in range(2):
                            mh, ml = t["m_hi"][:, 2 * i + j, :], t["m_lo"][:, 2 * i + j, :]
                            for m, (l, r) in enumerate(((mh, lat[0]), (mh, lat[1]), (ml, lat[0]))):
                                last = pe.matmul(psQ[:, j * AT:j * AT + AT], l, r, start=(m == 0), stop=(m == 2))
                        last.then_inc(s_qp, 1)
                    n, p2, u, there = unit(k, par, s + 2)
                    if there:
                        pe.wait_ge(s_mx, n + 1)
                        at_least(pe, s_mT, n)
                        pe.transpose(psM[:, 0:P], mx[u % 2][:, :], t["ident"][:, :]).then_inc(s_mp, 1)
                    n, p2, u, there = unit(k, par, s)
                    if there:
                        b = u % AB
                        pe.wait_ge(s_P, n + 1)
                        at_least(pe, s_On, n)
                        if s == 0:
                            pe.wait_ge(s_kvtok, k + 1)
                        for c in range(4):
                            o = 512 * (c // 2) + (D + 1) * (c % 2)
                            last = pe.matmul(psO[:, o:o + D + 1], pr[u % 2][:, c * P:c * P + P], kvtok[p2][:, b, 0:D + 1], start=True, stop=True)
                        last.then_inc(s_O, 1)
                    if s == 1 and front:
                        pe.wait_ge(s_kvs, 2 * (k + 2))
                        at_least(pe, s_ql, (k + 1) * UNITS)
                        for b in range(AB):
                            last = pe.transpose(psQ[:, b * P:b * P + P], kvs[:, b, :], t["ident"][:, :])
                        last.then_inc(s_kvp, 1)
                    n, p2, u, there = unit(k, par, s - 1)
                    if there:
                        pe.wait_ge(s_On, n + 1)
                        at_least(pe, s_OT, n)
                        if s == 1 and fin:
                            pe.wait_ge(s_h, k)
                        for c in range(4):
                            last = pe.transpose(psOT[:, c * P:c * P + P], on[u % 2][:, c, :], t["ident"][:, :])
                        last.then_inc(s_OTp, 1)
                    hd = (2 * s + 6) % HEADS
                    if core if s >= 5 else tail:
                        if s == 5:
                            pe.wait_ge(s_OTl, k * UNITS + 4)
                            at_least(pe, s_res, k)
                        if s == 1:
                            pe.wait_ge(s_OTl, k * UNITS)
                        for j in range(2):
                            nh, nl = t["n_hi"][:, hd + j, :], t["n_lo"][:, hd + j, :]
                            o_hi, o_lo = (o[:, hd + j, :, :].rearrange("p b q -> p (b q)") for o in (oh, ol))
                            for m, (l, r) in enumerate(((nh, o_hi), (nh, o_lo), (nl, o_hi))):
                                last = pe.matmul(psN[:, 0:AT], l, r, start=(hd + j == 0 and m == 0), stop=(hd + j == HEADS - 1 and m == 2))
                        last.then_inc(s_Np, 1)
            steady(pe, step)

        @block.scalar
        def _(act):
            def step(k, par):
                prep, front, core, tail, fin = active(k)
                for s in range(UNITS):
                    n, p2, u, there = unit(k, par, s + 1)
                    if there:
                        act.wait_ge(s_T, n + 1)
                        act.activation(pr[u % 2][:, :], psT[:, :], ACT.Exp).then_inc(s_P, 1)
                    n, p2, i, there = piece(k, par, s)
                    if there:
                        act.wait_ge(s_qp, n + 1)
                        act.activation(qh[p2][:, :, 2 * i:2 * i + 2, :].rearrange("p b j q -> p j b q"),
                                       psQ[:, :].rearrange("p (j b q) -> p j b q", j=2, b=AB), ACT.Copy).then_inc(s_qh, 1)
                    if s == 1 and front:
                        act.wait_ge(s_kvp, k + 2)
                        act.activation(kvh[1 - par][:, :], psQ[:, :], ACT.Copy).then_inc(s_kvh, 1)
                    n, p2, u, there = unit(k, par, s - 1)
                    if there:
                        b, g = u % AB, u // AB
                        src = psOT[:, :].rearrange("p (h q) -> p h q", q=SEQ)
                        act.wait_ge(s_OTp, n + 1)
                        at_least(act, s_OTl, n - 1)
                        act.activation(of[u % 2][:, :, :], src, ACT.Copy).then_inc(s_OTf, 1)
                        if b == 0:
                            at_least(act, s_Np, n - 4)
                        act.activation(oh[:, 8 * g:8 * g + 8, b, :], src, ACT.Copy).then_inc(s_OT, 1)
                    if s == 4 and tail:
                        act.wait_ge(s_Np, k * UNITS)
                        act.activation(res[:, :], psN[:, 0:AT], ACT.Copy).then_inc(s_res, 1)
            steady(act, step)

        @block.gpsimd
        def _(pl):
            for j in range(2):
                pl.memset(mx[j][:, :], 0.0).then_inc(s_init, 1)
                pl.memset(kvtok[j][:, :, D:D + 1], 1.0).then_inc(s_init, 1)
            pl.wait_ge(s_init, 4)

            def step(k, par):
                _, front, _, _, _ = active(k)
                if front:
                    scaled(k + 1, 1)
                for s in range(UNITS):
                    n, p2, u, there = unit(k, par, s - 1)
                    if there:
                        b, g = u % AB, u // AB
                        pl.wait_ge(s_OTf, n + 1)
                        pl.wait_ge(s_OT, n + 1)
                        pl.tensor_tensor(ol[:, 8 * g:8 * g + 8, b, :], of[u % 2][:, :, :],
                                         oh[:, 8 * g:8 * g + 8, b, :].bitcast(F32), ALU.subtract).then_inc(s_OTl, 1)
                    around(k, par, s)

            def around(k, par, s):
                prep, front, core, tail, fin = active(k)
                if s == 0 and front:
                    pl.wait_ge(s_kvs, 2 * (k + 2))
                    at_least(pl, s_O, k * UNITS)
                    pl.tensor_tensor(kvtok[1 - par][:, :, 0:D], kvg[:, :, :], t["shift"][:, :, :], ALU.add).then_inc(s_kvtok, 1)
                if s == 3 and fin:
                    pl.wait_ge(s_fmv, 2 * (k - 1))
                    pl.tensor_tensor(fve[:, :], fmv[:, :, 1], t["eps"][:, 0:2], ALU.add).then_inc(s_fve, 1)
                    pl.wait_ge(s_fve, k - 1)
                    pl.tensor_tensor(frs[:, :], fve[:, :], t["mhalf"][:, 0:2], ALU.pow).then_inc(s_frs, 1)
                if s == 4 and prep:
                    pl.wait_ge(s_mv, 4 * (k + 3))
                    pl.tensor_tensor(ve[:, :], mv[:, :, 1], t["eps"][:, 0:4], ALU.add).then_inc(s_ve, 1)
                    pl.wait_ge(s_ve, k + 3)
                    pl.tensor_tensor(rstd[:, :], ve[:, :], t["mhalf"][:, 0:4], ALU.pow).then_inc(s_rs, 1)
                if s == 7 and prep:
                    scaled(k + 2, 0)

            def scaled(q, half):
                two = slice(2 * half, 2 * half + 2)
                pl.wait_ge(s_kvn, 8 * q + 4 * half + 4)
                at_least(pl, s_kvtok, q)
                pl.tensor_tensor(kvg[:, two, :], kvn[:, two, :], t["gain"][:, two, :], ALU.mult).then_inc(s_kvg, 1)
                pl.wait_ge(s_kvg, 2 * q + half + 1)
                at_least(pl, s_kvp, q)
                pl.tensor_tensor(kvs[:, two, :], kvg[:, two, :], t["shift"][:, two, :], ALU.add).then_inc(s_kvs, 1)
            steady(pl, step)

        @block.vector
        def _(dve):
            dve.wait_ge(s_init, 4)
            dve.memset(spare[:, 0:1], 0.0).then_inc(s_h, 1)
            dve.memset(spare[:, 1:2], 0.0).then_inc(s_x2, 1)

            def step(k, par):
                prep, front, core, tail, fin = active(k)
                for s in range(UNITS):
                    if s == 3 and fin:
                        dve.wait_ge(s_fst, 2 * (k - 1))
                    if s == 4 and prep:
                        dve.wait_ge(s_st, 4 * (k + 3))
                    n, p2, u, there = unit(k, par, s + 2)
                    if there:
                        dve.wait_ge(s_S, n + 1)
                        dve.tensor_reduce(mx[u % 2][:, 0:4], psS[:, :].rearrange("p (c m) -> p c m", m=P), AX.X, ALU.max).then_inc(s_mx, 1)
                    if s == 3 and fin:
                        for i in range(2):
                            dve.bn_aggr(fmv[:, i, :], fst[:, i, :]).then_inc(s_fmv, 1)
                    if s == 4 and prep:
                        for i in range(4):
                            dve.bn_aggr(mv[:, i, :], st[:, i, :]).then_inc(s_mv, 1)
                    if s == 1 and fin:
                        dve.wait_ge(s_fp, k - 1)
                        dve.wait_ge(s_x2, 2 * (k - 2) + 1)
                        dve.tensor_tensor(h[:, :, :], psOT[:, 0:AT].rearrange("p (a b) -> p a b", b=D), dyn(xall, k - 2, 2), ALU.add).then_inc(s_h, 1)
                    n, p2, u, there = unit(k, par, s + 2)
                    if there:
                        dve.wait_ge(s_mp, n + 1)
                        dve.tensor_tensor(mT[u % 2][:, :, :], t["sel"][0:4, :, :],
                                          psM[0:4, 0:P].rearrange("p (o m) -> p o m", o=1).broadcast_to([4, 4, P]), ALU.mult).then_inc(s_mT, 1)
                    n, p2, i, there = piece(k, par, s)
                    if there:
                        dve.wait_ge(s_qh, n + 1)
                        v = lambda q: q[p2][:, :, 2 * i:2 * i + 2, :].rearrange("p b j q -> p j b q")
                        dve.tensor_tensor(v(ql), psQ[:, :].rearrange("p (j b q) -> p j b q", j=2, b=AB), v(qh).bitcast(F32),
                                          ALU.subtract).then_inc(s_ql, 1)
                    n, p2, u, there = unit(k, par, s)
                    if there:
                        dve.wait_ge(s_O, n + 1)
                        po = psO[:, :].rearrange("p (a r) -> p a r", a=2)[:, :, 0:2 * (D + 1)].rearrange("p a (j r) -> p a j r", j=2)
                        dve.reciprocal(rec[:, :].rearrange("p (a j) -> p a j", a=2), po[:, :, :, D]).then_inc(s_rc, 1)
                        dve.wait_ge(s_rc, n + 1)
                        dve.tensor_tensor(on[u % 2][:, :, :].rearrange("p (a j) d -> p a j d", a=2), po[:, :, :, 0:D],
                                          rec[:, :].rearrange("p (a j o) -> p a j o", a=2, o=1).broadcast_to([P, 2, 2, D]), ALU.mult).then_inc(s_On, 1)
                    if s == 1 and front:
                        dve.wait_ge(s_kvh, k + 2)
                        dve.tensor_tensor(kvl[1 - par][:, :], psQ[:, :], kvh[1 - par][:, :].bitcast(F32), ALU.subtract).then_inc(s_kvl, 1)
                    if s == 2 and fin:
                        dve.wait_ge(s_h, k)
                        for i in range(2):
                            dve.bn_stats(fst[:, i, :], h[:, i, :]).then_inc(s_fst, 1)
                    if s == 3 and prep:
                        dve.wait_ge(s_c[par], (k + 2 - par) * 16 + 32)
                        for i in range(2):
                            dve.bn_stats(st[:, i, :], dyn(xall, k * 2 + 4 + i)).then_inc(s_st, 1)
                        for i in range(2):
                            dve.bn_stats(st[:, 2 + i, :], cin[par][:, i, :]).then_inc(s_st, 1)
                    if s == 5 and fin:
                        dve.wait_ge(s_frs, k - 1)
                        for i in range(2):
                            dve.tensor_scalar(dyn(xall, k * 2 - 4 + i), h[:, i, :], fmv[:, i, 0:1], frs[:, i:i + 1],
                                              ALU.subtract, ALU.mult).then_inc(s_x2, 1)
                    if s >= 6 and prep:
                        i = s - 6
                        dve.wait_ge(s_rs, k + 3)
                        at_least(dve, s_kvg, 2 * (k + 2) - 1 + i)
                        for j in range(2):
                            r = slice(64 * j, 64 * j + 64)
                            dve.tensor_scalar(kvn[r, 2 * i + j, :], dyn(xall, k * 2 + 4 + i)[r], mv[r, i, 0:1], rstd[r, i:i + 1],
                                              ALU.subtract, ALU.mult).then_inc(s_kvn, 1)
                            dve.tensor_scalar(kvn[r, 2 * i + 1 - j, :], cin[par][r, i, :], mv[r, 2 + i, 0:1], rstd[r, 2 + i:3 + i],
                                              ALU.subtract, ALU.mult).then_inc(s_kvn, 1)
            steady(dve, step)


def router_phase(nc, t, w, xall, big, rows, xs_rows):
    G4 = 4
    NX = TILES // G4
    NW = 3 * E // G4
    with ExitStack() as ctx:
        a = Alloc(nc, ctx)
        x2h = a.sb("x2T_hi", [P, TOKENS], F32R)
        x2l = a.sb("x2T_lo", [P, TOKENS], F32R)
        raw = [a.sb(f"expert_raw{j}", [P, 3, G4, P]) for j in range(2)]
        logits = a.sb("logits", [P, TILES, E])
        top = a.sb("top", [P, TILES, 8])
        topi = a.sb("topi", [P, TILES, 8], U32)
        topf = a.sb("topf", [P, TILES, TOPK])
        dif = a.sb("dif", [P, TILES, TOPK])
        ex = a.sb("ex", [P, TILES, TOPK])
        sm = a.sb("sm", [P, TILES])
        rs = a.sb("rs", [P, TILES])
        iota_i = a.sb("iota_i", [P, E], I32)
        iota_e = a.sb("iota_e", [P, E])
        iota_ji = a.sb("iota_ji", [P, 2], I32)
        iota_j = a.sb("iota_j", [P, 2])
        oh = [a.sb(f"oh{k}", [P, TILES, E], BF16) for k in range(TOPK)]
        mask = [a.sb(f"mask{k}", [P, TILES, E], BF16) for k in range(TOPK - 1)]
        tri = a.sb("tri", [P, P], BF16)
        ones = a.sb("ones", [P, P], BF16)
        keep = [a.sb(f"keep_e{g}", [P, E, n]) for g, n in enumerate(SPLIT)]
        cnt = [a.sb(f"cnt{g}", [P, E, n]) for g, n in enumerate(SPLIT)]
        incl = [a.sb(f"incl{g}", [P, E, n]) for g, n in enumerate(SPLIT)]
        place = [a.sb(f"place{g}", [P, E, n]) for g, n in enumerate(SPLIT)]
        place2 = [a.sb(f"place2_{g}", [P, n, E]) for g, n in enumerate(SPLIT)]
        hit = [a.sb(f"hit{g}", [P, n, E]) for g, n in enumerate(SPLIT)]
        slotf = a.sb("slotf", [P, TOPK, TILES])
        tot1 = [a.sb(f"tot1{g}", [P, E], I32) for g in range(2)]
        tot2 = [a.sb(f"tot2{g}", [P, E], I32) for g in range(2)]
        nt = [a.sb(f"nt{g}", [P, E]) for g in range(2)]
        ends = [a.sb(f"ends{g}", [P, E]) for g in range(2)]
        onesE = a.sb("onesE", [P, E])
        base = [a.sb(f"base{g}", [P, E]) for g in range(2)]
        cmp_ = a.sb("cmp", [P, 2, E])
        eidp = a.sb("eidp", [P, 2])
        eidq = a.sb("eidq", [P, 2])
        sgs = [a.sb(f"sgs{j}", [P, MT]) for j in range(2)]
        hsT = [a.sb(f"hsT{j}", [P, 4, MT]) for j in range(2)]
        TB = [a.ps(f"r_TB{j}") for j in range(2)]
        LR = a.ps("r_LR", 1024)
        CC = a.ps("r_CC", 1024)
        EE = a.ps("r_EE")
        DD = a.ps("r_DD")
        s_raw = [a.sem(f"r_raw{j}") for j in range(2)]
        (s_fill, s_const, s_tp, s_ev, s_lo, s_lg, s_L, s_top, s_ti, s_dif, s_ex, s_w, s_f, s_oh, s_mk, s_rk, s_cnt, s_incl,
         s_tiles, s_pl, s_hit, s_sl, s_slot, s_ei, s_ee, s_sc, s_gp, s_sg, s_up, s_hs, s_dp, s_sh) = (
            a.sem("r_" + n) for n in ("fill", "const", "tp", "ev", "lo", "lg", "L", "top", "ti", "dif", "ex", "w", "f", "oh",
                                     "mk", "rk", "cnt", "incl", "tiles", "pl", "hit", "sl", "slot", "ei",
                                     "ee", "sc", "gp", "sg", "up", "hs", "dp", "sh"))
        block = ctx.enter_context(nc.Block())
        raws = [w[n].rearrange("(g i) h d -> g h i d", i=G4) for n in ("gate_w", "up_w", "down_w")]

        def weight_dst(g):
            e4, kind = g // 3 * G4, g % 3
            return big["wd"][:, e4:e4 + G4, :] if kind == 2 else big["wgu"][:, e4:e4 + G4, kind * P:kind * P + P]

        @block.sync
        def _(sp):
            for g in range(E // G4):
                if g >= 2:
                    sp.wait_ge(s_tp, NX + 3 * (g - 1))
                for kind in range(3):
                    sp.dma_start(raw[g % 2][:, kind], raws[kind][g]).then_inc(s_raw[g % 2], 16)

        @block.gpsimd
        def _(pl):
            pl.memset(ones[:, :], 1.0).then_inc(s_fill, 1)
            pl.memset(tri[:, :], 1.0).then_inc(s_fill, 1)
            for g in range(2):
                pl.memset(keep[g][:, :, :], 1.0).then_inc(s_fill, 1)
            pl.memset(onesE[:, :], 1.0).then_inc(s_fill, 1)
            pl.memset(big["eid"][:, 0:1], 0).then_inc(s_const, 1)
            pl.iota(iota_i[:, :], pattern=[[1, E]], base=0, channel_multiplier=0).then_inc(s_fill, 1)
            pl.iota(iota_ji[:, :], pattern=[[0, 2]], base=0, channel_multiplier=1).then_inc(s_fill, 1)
            pl.wait_ge(s_fill, 7)
            pl.affine_select(out=tri[:, :], in_=tri[:, :], compare_op=ALU.is_gt, fill=0.0, base=0, pattern=[[1, P]],
                             channel_multiplier=-1).then_inc(s_const, 1)
            for g in range(2):
                pl.memset(keep[g][:, :, 0:1], 0.0).then_inc(s_const, 1)
            pl.tensor_copy(iota_e[:, :], iota_i[:, :]).then_inc(s_const, 1)
            pl.tensor_copy(iota_j[:, :], iota_ji[:, :]).then_inc(s_const, 1)
            pl.wait_ge(s_slot, 1)
            scatter(pl, 0, rows, xall, xs_rows[0], s_sc)
            pl.wait_ge(s_sc, 16 * SPLIT[0] * TOPK)

        @block.tensor
        def _(pe):
            def logit_group(g):
                pe.wait_ge(s_lo, g + 1)
                for i in range(G4 * g, G4 * g + G4):
                    out = (LR, CC)[i // 16][:, i % 16 * 2 * E:(i % 16 + 1) * 2 * E]
                    xh, xl = (x[:, i * P:i * P + P] for x in (x2h, x2l))
                    pe.matmul(out, xh, t["rT"][:, :, 0:E], start=True, stop=False, skip_group_check=True)
                    last = pe.matmul(out[:, 0:E], xl, t["rT"][:, 0, 0:E], start=False, stop=True, skip_group_check=True)
                last.then_inc(s_lg, 1)

            for g in range(NX):
                if g >= 2:
                    pe.wait_ge(s_lo, g - 1)
                for i in range(G4):
                    last = pe.transpose(TB[g % 2][:, i * P:i * P + P], xall[:, G4 * g + i, :], t["ident"][:, :])
                last.then_inc(s_tp, 1)
                if g >= 1:
                    logit_group(g - 1)
            logit_group(NX - 1)
            m = mask[2][:, :, :].rearrange("p t e -> p (t e)")
            for grp in range(2):
                for g in range(grp * NW // 2, (grp + 1) * NW // 2):
                    pe.wait_ge(s_raw[g // 3 % 2], 48 * (g // 3 // 2 + 1))
                    pe.wait_ge(s_ev, NX + g - 1)
                    for i in range(G4):
                        last = pe.transpose(TB[g % 2][:, i * P:i * P + P], raw[g // 3 % 2][:, g % 3, i, :], t["ident"][:, :])
                    last.then_inc(s_tp, 1)
                pe.wait_ge(s_const, 6)
                pe.wait_ge(s_mk, 3 * grp + 3)
                at_least(pe, s_pl, 3 * grp)
                lo, hi = FIRST[grp] * E, (FIRST[grp] + SPLIT[grp]) * E
                for o in (0, 512):
                    b, e = max(lo, o), min(hi, o + 512)
                    if b < e:
                        pe.matmul(LR[:, b:e], tri[:, :], m[:, b:e], start=True, stop=True)
                        last = pe.matmul(CC[:, b:e], ones[:, :], m[:, b:e], start=True, stop=True)
                last.then_inc(s_rk, 1)
            pe.wait_ge(s_ev, NX + NW)
            pe.wait_ge(s_pl, 6)

            def product(out, wt, c, xh, xl):
                wh, wl = (x[:, c * P:c * P + P] for x in wt)
                for m, (l, r) in enumerate(((wh, xh), (wh, xl), (wl, xh))):
                    last = pe.matmul(out, l, r, start=(m == 0), stop=(m == 2))
                return last

            def step(k):
                xh, xl = (x[:, bass.ds(k * MT, MT)] for x in (x2h, x2l))
                for c in range(4):
                    at_least(pe, s_sg, k * 4 + c - 1)
                    product(TB[c % 2][:, :], t["sgT"], c, xh, xl).then_inc(s_gp, 1)
                    at_least(pe, s_hs, k * 4 + c - 1)
                    product(CC[:, c % 2 * 512:c % 2 * 512 + 512], t["suT"], c, xh, xl).then_inc(s_up, 1)

            def down(k, par):
                pe.wait_ge(s_hs, k * 4 + 4)
                at_least(pe, s_sh, k)
                for i in range(4):
                    for c in range(4):
                        last = pe.matmul(DD[:, i * P:i * P + P], hsT[par][:, c, i * P:i * P + P], t["sdT"][:, c, :], start=(c == 0), stop=(c == 3))
                last.then_inc(s_dp, 1)
            step(0)
            pe.wait_ge(s_ei, 4)
            for g in range(2):
                last = pe.matmul(EE[0:1, g * P:g * P + P], eidq[:, g:g + 1], t["ident"][:, :], start=True, stop=True)
            last.then_inc(s_ee, 1)
            step(1)
            down(0, 0)
            with pe.Fori(1, NX // 2) as i:
                step(i * 2)
                down(i * 2 - 1, 1)
                step(i * 2 + 1)
                down(i * 2, 0)
            down(NX - 1, 1)

        @block.scalar
        def _(act):
            for g in range(NX):
                act.wait_ge(s_tp, g + 1)
                act.activation(x2h[:, g * MT:g * MT + MT], TB[g % 2][:, :], ACT.Copy).then_inc(s_ev, 1)
            for g in range(NW):
                act.wait_ge(s_tp, NX + g + 1)
                act.activation(weight_dst(g), TB[g % 2][:, :].rearrange("p (i m) -> p i m", m=P), ACT.Copy).then_inc(s_ev, 1)
            act.wait_ge(s_dif, 2)
            act.activation(ex[:, :, :], dif[:, :, :], ACT.Exp).then_inc(s_ex, 1)

            def step(k, par):
                for c in range(4):
                    act.wait_ge(s_gp, k * 4 + c + 1)
                    at_least(act, s_hs, k * 4 + c - 1)
                    act.activation(sgs[c % 2][:, :], TB[c % 2][:, :], ACT.Silu).then_inc(s_sg, 1)
            step(0, 0)
            step(1, 1)
            with act.Fori(1, NX // 2) as i:
                step(i * 2, 0)
                step(i * 2 + 1, 1)

        @block.vector
        def _(dve):
            bt = lambda ap, shape: ap.broadcast_to(shape)
            for g in range(NX):
                dve.wait_ge(s_ev, g + 1)
                cols = slice(g * MT, g * MT + MT)
                dve.tensor_tensor(x2l[:, cols], TB[g % 2][:, :], x2h[:, cols].bitcast(F32), ALU.subtract).then_inc(s_lo, 1)
            dve.wait_ge(s_lg, NX)
            half = [P, TILES // 2, E]
            for j, part in enumerate((LR, CC)):
                both = part[:, :].rearrange("p (t h e) -> p t h e", h=2, e=E)
                mine = logits[:, j * TILES // 2:(j + 1) * TILES // 2, :]
                dve.tensor_tensor(mine, both[:, :, 0, :], bt(t["rbias"][:, :].rearrange("p (o e) -> p o e", o=1), half), ALU.add).then_inc(s_L, 1)
                dve.wait_ge(s_L, 2 * j + 1)
                dve.tensor_tensor(mine, mine, both[:, :, 1, :], ALU.add).then_inc(s_L, 1)
            dve.wait_ge(s_L, 4)

            def route(g):
                T0, n = FIRST[g], SPLIT[g]
                tl = slice(T0, T0 + n)
                NE = [P, n, E]
                for i in range(T0, T0 + n):
                    dve.max(top[:, i, :], logits[:, i, :]).then_inc(s_top, 1)
                for i in range(T0, T0 + n):
                    dve.wait_ge(s_top, i + 1)
                    dve.max_index(topi[:, i, :], top[:, i, :], logits[:, i, :]).then_inc(s_ti, 1)
                dve.wait_ge(s_top, T0 + n)
                dve.tensor_tensor(dif[:, tl, :], top[:, tl, 0:TOPK], bt(top[:, tl, 0:1], [P, n, TOPK]), ALU.subtract).then_inc(s_dif, 1)
                dve.wait_ge(s_ti, T0 + n)
                dve.tensor_copy(topf[:, tl, :], topi[:, tl, 0:TOPK]).then_inc(s_f, 1)
                dve.wait_ge(s_const, 6)
                dve.wait_ge(s_f, g + 1)
                for k in range(TOPK):
                    dve.tensor_tensor(oh[k][:, tl, :], bt(iota_e[:, :].rearrange("p (o e) -> p o e", o=1), NE), bt(topf[:, tl, k:k + 1], NE),
                                      ALU.is_equal).then_inc(s_oh, 1)
                src = oh[0]
                for k in range(1, TOPK):
                    dve.wait_ge(s_oh, g * TOPK + k + 1)
                    if k > 1:
                        dve.wait_ge(s_mk, g * 3 + k - 1)
                    dve.tensor_tensor(mask[k - 1][:, tl, :], src[:, tl, :], oh[k][:, tl, :], ALU.add).then_inc(s_mk, 1)
                    src = mask[k - 1]
                dve.wait_ge(s_rk, g + 1)
                dve.tensor_copy(cnt[g][:, :, :], CC[:, T0 * E:(T0 + n) * E].rearrange("p (t e) -> p e t", e=E)).then_inc(s_cnt, 1)
                dve.wait_ge(s_cnt, g + 1)
                flat = lambda z: z[:, :, :].rearrange("p e t -> p (e t)")
                dve.tensor_tensor_scan(flat(incl[g]), flat(keep[g]), flat(cnt[g]), 0.0, ALU.mult, ALU.add).then_inc(s_incl, 1)
                dve.wait_ge(s_incl, g + 1)
                dve.tensor_scalar(tot1[g][:, :], incl[g][:, :, n - 1], float(P - 1), None, ALU.add).then_inc(s_tiles, 1)
                dve.wait_ge(s_tiles, 5 * g + 1)
                dve.tensor_scalar(tot2[g][:, :], tot1[g][:, :], 7, None, ALU.arith_shift_right).then_inc(s_tiles, 1)
                dve.wait_ge(s_tiles, 5 * g + 2)
                dve.tensor_copy(nt[g][:, :], tot2[g][:, :]).then_inc(s_tiles, 1)
                dve.wait_ge(s_tiles, 5 * g + 3)
                dve.tensor_tensor_scan(ends[g][:, :], onesE[:, :], nt[g][:, :], 0.0, ALU.mult, ALU.add).then_inc(s_tiles, 1)
                dve.wait_ge(s_tiles, 5 * g + 4)
                dve.tensor_tensor(base[g][:, :], ends[g][:, :], nt[g][:, :], ALU.subtract).then_inc(s_tiles, 1)
                dve.tensor_tensor(place[g][:, :, :], incl[g][:, :, :], cnt[g][:, :, :], ALU.subtract).then_inc(s_pl, 1)
                dve.wait_ge(s_tiles, 5 * g + 5)
                dve.wait_ge(s_pl, 3 * g + 1)
                dve.scalar_tensor_tensor(out=incl[g][:, :, :], in0=bt(base[g][:, :].rearrange("p (e o) -> p e o", o=1), [P, E, n]),
                                         scalar=float(P), in1=place[g][:, :, :], op0=ALU.mult, op1=ALU.add).then_inc(s_pl, 1)
                dve.wait_ge(s_pl, 3 * g + 2)
                dve.tensor_tensor(place2[g][:, :, :], LR[:, T0 * E:(T0 + n) * E].rearrange("p (t e) -> p t e", e=E),
                                  incl[g][:, :, :].rearrange("p e t -> p t e"), ALU.add).then_inc(s_pl, 1)
                dve.wait_ge(s_pl, 3 * g + 3)
                for k in range(TOPK):
                    at_least(dve, s_sl, g * TOPK + k)
                    dve.tensor_tensor(hit[g][:, :, :], oh[k][:, tl, :], place2[g][:, :, :], ALU.mult).then_inc(s_hit, 1)
                    dve.wait_ge(s_hit, g * TOPK + k + 1)
                    dve.tensor_reduce(slotf[:, k, tl], hit[g][:, :, :], AX.X, ALU.add).then_inc(s_sl, 1)
                dve.wait_ge(s_sl, (g + 1) * TOPK)
                dve.tensor_copy(rows[:, :, tl], slotf[:, :, tl]).then_inc(s_slot, 1)
            for g in range(2):
                route(g)
            for g in range(2):
                dve.tensor_scalar(cmp_[:, g, :], ends[g][:, :], iota_j[:, g:g + 1], None, ALU.is_le).then_inc(s_ei, 1)
            dve.wait_ge(s_ei, 2)
            dve.tensor_reduce(eidp[:, :], cmp_[:, :, :], AX.X, ALU.add).then_inc(s_ei, 1)
            dve.wait_ge(s_ei, 3)
            dve.tensor_scalar(eidq[:, :], eidp[:, :], float(E - 1), None, ALU.min).then_inc(s_ei, 1)
            dve.wait_ge(s_ex, 1)
            dve.tensor_reduce(sm[:, :], ex[:, :, :], AX.X, ALU.add).then_inc(s_w, 1)
            dve.wait_ge(s_w, 1)
            dve.reciprocal(rs[:, :], sm[:, :]).then_inc(s_w, 1)
            dve.wait_ge(s_w, 2)
            dve.tensor_tensor(big["wts"][:, :, :], ex[:, :, :], bt(rs[:, :].rearrange("p (t o) -> p t o", o=1), [P, TILES, TOPK]), ALU.mult).then_inc(s_w, 1)

            def step(k, par):
                for c in range(4):
                    dve.wait_ge(s_sg, k * 4 + c + 1)
                    dve.wait_ge(s_up, k * 4 + c + 1)
                    if c == 0:
                        at_least(dve, s_dp, k - 1)
                    dve.tensor_tensor(hsT[par][:, c, :], sgs[c % 2][:, :], CC[:, c % 2 * 512:c % 2 * 512 + 512], ALU.mult).then_inc(s_hs, 1)

            def down(k):
                dve.wait_ge(s_dp, k + 1)
                dve.tensor_tensor(dyn(big["sh"], k, 4), DD[:, :].rearrange("p (a b) -> p a b", b=D), dyn(xall, k, 4), ALU.add).then_inc(s_sh, 1)
            step(0, 0)
            dve.wait_ge(s_ee, 1)
            for g in range(2):
                dve.tensor_copy(big["eid"][:, 1 + g * XTG[0]:1 + g * XTG[0] + XTG[g]], EE[0:1, g * P:g * P + XTG[g]]).then_inc(s_ei, 1)
            step(1, 1)
            down(0)
            with dve.Fori(1, NX // 2) as i:
                step(i * 2, 0)
                down(i * 2 - 1)
                step(i * 2 + 1, 1)
                down(i * 2)
            down(NX - 1)


def scatter(pl, g, rows, xall, xs_rows, s_sc):
    for i in range(FIRST[g], FIRST[g] + SPLIT[g]):
        for k in range(TOPK):
            pl.indirect_dma_start(xs_rows[:, :], bass.IndirectOffsetOnAxis(ap=rows[:, k, i:i + 1], axis=0),
                                  xall[:, i, :], None).then_inc(s_sc, 16)


WG = 4
EARLY = 3


def weigh(dve, big, rows_of, g, k, j, s_acc, first):
    i = g * WG + j
    total = dyn(big["sh"], i)
    if k:
        dve.wait_ge(s_acc, k * WG + j + 1 - WG + (g - first) * WG * TOPK)
    dve.scalar_tensor_tensor(out=total, in0=rows_of(i, k), scalar=big["wts"][:, i, k:k + 1], in1=total,
                             op0=ALU.mult, op1=ALU.add).then_inc(s_acc, 1)


def gather(pl, i, rows, y_rows, dst, s_got):
    for k in range(TOPK):
        pl.indirect_dma_start(dst[:, k, :], None, y_rows[:, :],
                              bass.IndirectOffsetOnAxis(ap=rows[:, k, i:i + 1], axis=0)).then_inc(s_got, 16)


def experts_phase(nc, t, big, rows, xall, xs_rows, y_rows):
    G4 = 4
    NB = TS // G4
    NS = XT // TS
    NS0 = XTG[0] // TS
    xs_g = [r.rearrange("(g i p) d -> g p i d", i=G4, p=P) for r in xs_rows]
    y_g = [r.rearrange("(g i p) d -> g p i d", i=G4, p=P) for r in y_rows]
    with ExitStack() as ctx:
        a = Alloc(nc, ctx)
        xj = [a.sb(f"xj{j}", [P, G4, D]) for j in range(NB)]
        yj = [a.sb(f"yj{j}", [P, G4, D]) for j in range(NB)]
        xT = [a.sb(f"xjT{j}", [P, P]) for j in range(2)]
        sj = [a.sb(f"silu{j}", [P, P]) for j in range(2)]
        hj = [a.sb(f"hid{j}", [P, P]) for j in range(2)]
        hT = [a.sb(f"hidT{j}", [P, P]) for j in range(2)]
        psX, psG, psH, psY = ([a.ps(f"e_{n}{j}") for j in range(2)] for n in "XGHY")
        s_ld = [a.sem(f"e_ld{j}") for j in range(NB)]
        s_st = [a.sem(f"e_st{j}") for j in range(NB)]
        s_xp, s_x, s_g, s_si, s_h, s_hp, s_hT, s_yp, s_y, s_sc, s_acc = (
            a.sem("e_" + n) for n in ("xp", "x", "g", "si", "h", "hp", "hT", "yp", "y", "sc", "acc"))
        s_got = [a.sem(f"e_got{j}") for j in range(EARLY + 1)]
        block = ctx.enter_context(nc.Block())

        def steady(eng, step):
            step(-1)
            step(0)
            with eng.Fori(1, NS - 1) as i:
                step(i)
            step(NS - 1)
            step(NS)

        def tile(k, s):
            n = k * TS + s
            first = k + s // TS
            return n, s % TS, not isinstance(k, int) or 0 <= first < NS

        @block.sync
        def _(sp):
            def step(k, load, store):
                for j in range(NB):
                    if load is not None:
                        at_least(sp, s_xp, k * TS + G4 * (j + 1))
                        src = xs_g[load][bass.ds((k + (1 - NS0 * load)) * NB + j, 1)]
                        sp.dma_start(xj[j][:, :, :], src.rearrange("a p i d -> p (a i) d")).then_inc(s_ld[j], 16)
                    if store is not None:
                        sp.wait_ge(s_y, k * TS + G4 * (j + 1))
                        dst = y_g[store][bass.ds((k - NS0 * store) * NB + j, 1)]
                        sp.dma_start(dst.rearrange("a p i d -> p (a i) d"), yj[j][:, :, :]).then_inc(s_st[j], 16)
            step(-1, 0, None)
            with sp.Fori(0, NS0 - 1) as i:
                step(i, 0, 0)
            sp.wait_ge(s_sc, 16 * TOPK * SPLIT[1])
            step(NS0 - 1, 1, 0)
            with sp.Fori(NS0, NS - 1) as i:
                step(i, 1, 1)
            step(NS - 1, None, 1)
            for j in range(NB):
                sp.wait_ge(s_st[j], 16 * NS)

        @block.gpsimd
        def _(pl):
            scatter(pl, 1, rows, xall, xs_rows[1], s_sc)
            for j in range(NB):
                pl.wait_ge(s_st[j], 16 * NS0)
            for i in range(SPLIT[0]):
                gather(pl, i, rows, y_rows[0], big["got"][:, i * TOPK:(i + 1) * TOPK, :], s_got[min(i // WG, EARLY)])
            pl.wait_ge(s_got[EARLY], 16 * TOPK * (SPLIT[0] - EARLY * WG))

        @block.tensor
        def _(pe):
            def step(k):
                before = isinstance(k, int) and k < 0
                first, count = (0, 2) if before else (k * TS - 1, TS + 3)
                if isinstance(k, int) and k >= NS - 1:
                    count = TS + 1 if k < NS else 1
                _, ids = nc.values_load_multi_w_load_instructions(
                    big["eid"][0:1, bass.ds(first + 1, count)], engines=[mybir.EngineType.PE], min_val=0, max_val=E - 1,
                    skip_runtime_bounds_check_because="the router keeps them in 0 .. E-1")

                def expert(n, s):
                    return ids[s - TS if before else s + 1]
                for s in range(TS):
                    n, u, there = tile(k, s + 3)
                    if there:
                        if u % G4 == 0:
                            pe.wait_ge(s_ld[u // G4], (n - u) * (16 // TS) + 16)
                        at_least(pe, s_x, n - 1)
                        pe.transpose(psX[u % 2][:, 0:P], xj[u // G4][:, u % G4, :], t["ident"][:, :]).then_inc(s_xp, 1)
                    n, u, there = tile(k, s + 2)
                    if there:
                        e = expert(n, s + 2)
                        pe.wait_ge(s_x, n + 1)
                        at_least(pe, s_h, n - 1)
                        pe.matmul(psG[u % 2][:, 0:2 * P], xT[u % 2][:, :], dyn(big["wgu"], e), start=True, stop=True).then_inc(s_g, 1)
                    n, u, there = tile(k, s)
                    if there:
                        pe.wait_ge(s_h, n + 1)
                        at_least(pe, s_hT, n - 1)
                        pe.transpose(psH[u % 2][:, 0:P], hj[u % 2][:, :], t["ident"][:, :]).then_inc(s_hp, 1)
                    n, u, there = tile(k, s - 1)
                    if there:
                        e = expert(n, s - 1)
                        pe.wait_ge(s_hT, n + 1)
                        at_least(pe, s_y, n - 1)
                        pe.matmul(psY[u % 2][:, 0:P], hT[u % 2][:, :], dyn(big["wd"], e), start=True, stop=True).then_inc(s_yp, 1)
            steady(pe, step)

        @block.scalar
        def _(act):
            def step(k):
                for s in range(TS):
                    n, u, there = tile(k, s + 3)
                    if there:
                        act.wait_ge(s_xp, n + 1)
                        at_least(act, s_g, n - 1)
                        act.activation(xT[u % 2][:, :], psX[u % 2][:, 0:P], ACT.Copy).then_inc(s_x, 1)
                    n, u, there = tile(k, s + 2)
                    if there:
                        act.wait_ge(s_g, n + 1)
                        at_least(act, s_h, n - 1)
                        act.activation(sj[u % 2][:, :], psG[u % 2][:, 0:P], ACT.Silu).then_inc(s_si, 1)
                    n, u, there = tile(k, s - 1)
                    if there:
                        act.wait_ge(s_yp, n + 1)
                        if u % G4 == 0:
                            at_least(act, s_st[u // G4], (n - u) * (16 // TS))
                        act.activation(yj[u // G4][:, u % G4, :], psY[u % 2][:, 0:P], ACT.Copy).then_inc(s_y, 1)
            steady(act, step)

        @block.vector
        def _(dve):
            rows_of = lambda i, k: big["got"][:, i * TOPK + k, :]

            def step(k):
                g = k - (NS - EARLY) if isinstance(k, int) and NS - EARLY <= k < NS else None
                if g is not None:
                    dve.wait_ge(s_got[g], 16 * TOPK * WG)
                for s in range(TS):
                    if g is not None:
                        weigh(dve, big, rows_of, g, s // WG, s % WG, s_acc, 0)
                    n, u, there = tile(k, s)
                    if there:
                        dve.wait_ge(s_hp, n + 1)
                        at_least(dve, s_yp, n - 1)
                        dve.tensor_copy(hT[u % 2][:, :], psH[u % 2][:, 0:P]).then_inc(s_hT, 1)
                    n, u, there = tile(k, s + 2)
                    if there:
                        dve.wait_ge(s_si, n + 1)
                        at_least(dve, s_hp, n - 1)
                        dve.tensor_tensor(hj[u % 2][:, :], sj[u % 2][:, :], psG[u % 2][:, P:2 * P], ALU.mult).then_inc(s_h, 1)
            step(-1)
            step(0)
            with dve.Fori(1, NS - EARLY) as i:
                step(i)
            for k in range(NS - EARLY, NS + 1):
                step(k)


def combine_phase(nc, t, big, rows, y_rows, out):
    G4 = 4
    NG = TILES // G4
    out_g = out.rearrange("(g i p) d -> g p i d", i=G4, p=P)
    with ExitStack() as ctx:
        a = Alloc(nc, ctx)
        got = [a.sb(f"got{j}", [P, TOPK, D]) for j in range(SPLIT[1])]
        st = [a.sb(f"c_st{j}", [P, G4, 6]) for j in range(2)]
        mv = [a.sb(f"c_mv{j}", [P, G4, 2]) for j in range(2)]
        sd = [a.sb(f"c_sd{j}", [P, G4]) for j in range(2)]
        rstd = [a.sb(f"c_rstd{j}", [P, G4]) for j in range(2)]
        ob = [a.sb(f"ob{j}", [P, G4, D]) for j in range(2)]
        s_got = [a.sem(f"c_got{j}") for j in range(SPLIT[1] // G4)]
        s_o = [a.sem(f"c_o{j}") for j in range(2)]
        s_acc, s_st, s_mv, s_sd, s_rs, s_ob = (a.sem("c_" + n) for n in ("acc", "st", "mv", "sd", "rs", "ob"))
        block = ctx.enter_context(nc.Block())

        @block.gpsimd
        def _(pl):
            for j in range(SPLIT[1]):
                gather(pl, FIRST[1] + j, rows, y_rows[1], got[j], s_got[j // G4])

        @block.scalar
        def _(act):
            for g in range(NG):
                act.wait_ge(s_mv, G4 * (g + 1))
                if g >= 2:
                    act.wait_ge(s_rs, g - 1)
                act.activation(sd[g % 2][:, :], mv[g % 2][:, :, 1], ACT.Sqrt, bias=t["eps"][:, 0:1]).then_inc(s_sd, 1)

        @block.vector
        def _(dve):
            def rows_of(i, k):
                return got[i - FIRST[1]][:, k, :] if i >= FIRST[1] else big["got"][:, i * TOPK + k, :]

            def sums(g, par):
                if g >= EARLY:
                    if g * WG >= FIRST[1]:
                        dve.wait_ge(s_got[g - FIRST[1] // WG], 16 * TOPK * WG)
                    for k in range(TOPK):
                        for j in range(WG):
                            weigh(dve, big, rows_of, g, k, j, s_acc, EARLY)
                    dve.wait_ge(s_acc, (g - EARLY + 1) * WG * TOPK)
                for j in range(G4):
                    dve.bn_stats(st[par][:, j, :], dyn(big["sh"], g * G4 + j)).then_inc(s_st, 1)

            def norm(g, par):
                dve.wait_ge(s_sd, g + 1)
                dve.reciprocal(rstd[par][:, :], sd[par][:, :]).then_inc(s_rs, 1)
                dve.wait_ge(s_rs, g + 1)
                at_least(dve, s_o[par], (g - par) * 8)
                for j in range(G4):
                    dve.tensor_scalar(ob[par][:, j, :], dyn(big["sh"], g * G4 + j), mv[par][:, j, 0:1], rstd[par][:, j:j + 1],
                                      ALU.subtract, ALU.mult).then_inc(s_ob, 1)

            def aggregate(g, par):
                for j in range(G4):
                    dve.bn_aggr(mv[par][:, j, :], st[par][:, j, :]).then_inc(s_mv, 1)
            for g in range(NG):
                sums(g, g % 2)
                dve.wait_ge(s_st, G4 * (g + 1))
                aggregate(g, g % 2)
                if g >= 1:
                    norm(g - 1, (g - 1) % 2)
            norm(NG - 1, (NG - 1) % 2)

        @block.sync
        def _(sp):
            for g in range(NG):
                sp.wait_ge(s_ob, G4 * (g + 1))
                sp.dma_start(out_g[g], ob[g % 2][:, :, :]).then_inc(s_o[g % 2], 16)
            for j in range(2):
                sp.wait_ge(s_o[j], 16 * NG // 2)


def decoder(nc, x, ctx_in, w, out, stop_after=None):
    xf = x.rearrange("b s d -> (b s) d")
    outf = out.rearrange("b s d -> (b s) d")
    with ExitStack() as ctx:
        a = Alloc(nc, ctx)
        t = {
            "ident": a.sb("ident", [P, P]), "mhalf": a.sb("mhalf", [P, 8]),
            "one": a.sb("one", [P, 4]), "eps": a.sb("eps", [P, 8]),
            "rbias": a.sb("rbias", [P, E]),
            "sgT": [a.sb("sgT_hi", [P, HS], F32R), a.sb("sgT_lo", [P, HS], F32R)],
            "suT": [a.sb("suT_hi", [P, HS], F32R), a.sb("suT_lo", [P, HS], F32R)],
            "rT": a.sb("rT", [P, 2, P], F32R),
            "sdT": a.sb("sdT", [P, 4, P]),
        }
        xs_rows = [nc.dram_tensor(f"xs_rows{g}", [XTG[g] * P, D], F32, kind="Internal").ap() for g in range(2)]
        y_rows = [nc.dram_tensor(f"y_rows{g}", [XTG[g] * P, D], F32, kind="Internal").ap() for g in range(2)]
        xall = a.sb("xall", [P, TILES, D])
        with ExitStack() as heads:
            b = Alloc(nc, heads)
            for name, dt in (("m_hi", F32R), ("m_lo", F32R), ("n_hi", F32R), ("n_lo", F32R)):
                t[name] = b.sb(name, [P, HEADS, P], dt)
            t["gain"], t["shift"], t["sel"] = (b.sb(n, [P, AB, P]) for n in ("gain", "shift", "sel"))
            t["ones_r"] = b.sb("ones_r", [P, P], F32R)
            with ExitStack() as mixer:
                m = Alloc(nc, mixer)
                for name, shape in (("winT", [P, 2 * DI]), ("aT", [P, 2, DI]), ("bT", [P, 2, DI])):
                    t[name] = [m.sb(name + part, shape, F32R) for part in ("_hi", "_lo")]
                for name, shape in (("wdtT", [P, 2, DI]), ("cW", [P, 2, DI]), ("woT", [P, 2, P]), ("conv_w", [P, 2, 3]), ("conv_b", [P, 2])):
                    t[name] = m.sb(name if "conv" not in name else name + "_sb", shape)
                setup_phase(nc, t, w)
                mixer_phase(nc, t, w, xf, xall, xs_rows)
            attention_phase(nc, t, ctx_in, xall)
        if stop_after:
            with ExitStack() as c2:
                s = Alloc(nc, c2).sem("s_dbg")
                block = c2.enter_context(nc.Block())

                @block.sync
                def _(sp):
                    sp.dma_start(outf.rearrange("(t p) d -> p t d", p=P), xall[:, :, :]).then_inc(s, 16)
                    sp.wait_ge(s, 16)
            return
        big = {
            "wgu": a.sb("wgu", [P, E, 2 * P]), "wd": a.sb("wd", [P, E, P]), "sh": a.sb("sh", [P, TILES, D]),
            "wts": a.sb("wts", [P, TILES, TOPK]), "eid": a.sb("eid", [1, 2 * P], I32),
        }
        rows = a.sb("rows", [P, TOPK, TILES], U32)
        router_phase(nc, t, w, xall, big, rows, xs_rows)
        big["got"] = a.sb("got", [P, TOPK * SPLIT[0], D])
        experts_phase(nc, t, big, rows, xall, xs_rows, y_rows)
        combine_phase(nc, t, big, rows, y_rows, outf)


_INS = ['x', 'ctx_1024', 'L0_attn_W_in', 'L0_attn_conv_w', 'L0_attn_conv_b', 'L0_attn_W_dt', 'L0_attn_A_proj', 'L0_attn_B_proj',
        'L0_attn_C_proj', 'L0_attn_W_out', 'L0_xattn_ln_m_g', 'L0_xattn_ln_m_b', 'L0_xattn_ln_l_g', 'L0_xattn_ln_l_b',
        'L0_xattn_Wq', 'L0_xattn_Wkv', 'L0_xattn_Wout', 'L0_ffn_router_w', 'L0_ffn_router_bias', 'L0_ffn_gate_w', 'L0_ffn_up_w',
        'L0_ffn_down_w', 'L0_ffn_sgate_w', 'L0_ffn_sup_w', 'L0_ffn_sdown_w']
STOP = None


def kernel(**inputs):
    import concourse.bacc as _bacc
    from concourse.bass_utils import run_bass_kernel_spmd as _run

    nc = _bacc.Bacc("TRN2", target_bir_lowering=False, num_devices=1)
    arrays, aps = {}, {}
    for name in _INS:
        arr = np.ascontiguousarray(inputs[name])
        arrays[f"in_{name}_dram"] = arr
        short = name.replace("L0_attn_", "").replace("L0_xattn_", "").replace("L0_ffn_", "")
        aps[short] = nc.dram_tensor(f"in_{name}_dram", arr.shape, mybir.dt.from_np(arr.dtype), kind="ExternalInput").ap()
    out = nc.dram_tensor("out_0_dram", (BATCH, SEQ, D), F32, kind="ExternalOutput").ap()
    decoder(nc, aps.pop("x"), aps.pop("ctx_1024"), aps, out, STOP)
    r = _run(nc, [arrays], core_ids=[0])
    return r.results[0]["out_0_dram"]
```
